# Optimizing a Trainium2 kernel written in Bass

```python
import numpy as np
import jax
import jax.numpy as jnp

def _softmax(x, axis=-1):
    return jax.nn.softmax(x, axis=axis)

def _gelu(x):
    return jax.nn.gelu(x, approximate=True)

def _silu(x):
    return jax.nn.silu(x)

def _sigmoid(x):
    return jax.nn.sigmoid(x)

def _layernorm(x, axis=-1, eps=1e-05):
    m = jnp.mean(x, axis=axis, keepdims=True)
    v = jnp.var(x, axis=axis, keepdims=True)
    return (x - m) / jnp.sqrt(v + eps)

def _scatter_add(tgt, idx, src, axis=0):
    return tgt.at[idx].add(src)

def _segment_sum(src, seg, n):
    return jax.ops.segment_sum(src, seg, n)
kernel_name = 'mk_macaron_d1_jaxref_r8_e3f896'

def setup_inputs(seed: int=0):
    np.random.seed(seed)
    _w = jnp.asarray

    def _L0_attn_setup():
        import jax, jax.numpy as jnp
        import numpy as np
        B, S, HID = (2, 256, 128)
        NH = 16
        HD = HID // NH
        BASE = 10000.0

        def rotate_half(x):
            x1, x2 = jnp.split(x, 2, axis=-1)
            return jnp.concatenate((-x2, x1), axis=-1)
        key = jax.random.key(seed)
        ks = jax.random.split(key, 9)
        sc = 1.0 / np.sqrt(HID)
        inp = {'x': jax.random.normal(ks[0], (B, S, HID), dtype=jnp.float32), 'wq': jax.random.normal(ks[1], (HID, HID), dtype=jnp.float32) * sc, 'bq': jnp.zeros((HID,), dtype=jnp.float32), 'wk': jax.random.normal(ks[2], (HID, HID), dtype=jnp.float32) * sc, 'bk': jnp.zeros((HID,), dtype=jnp.float32), 'wv': jax.random.normal(ks[3], (HID, HID), dtype=jnp.float32) * sc, 'bv': jnp.zeros((HID,), dtype=jnp.float32), 'wo': jax.random.normal(ks[4], (HID, HID), dtype=jnp.float32) * sc, 'bo': jnp.zeros((HID,), dtype=jnp.float32)}
        return inp
    _L0_attn_in = _L0_attn_setup()

    def _L0_ffn_setup():
        import jax, jax.numpy as jnp
        import numpy as np
        EPS = 1e-06
        LN_EPS = 1e-05

        def _absmean_core(W):
            gamma = jnp.mean(jnp.abs(W)) + EPS
            Ws = W / gamma
            Wq = jnp.sign(Ws) * jnp.minimum(jnp.round(jnp.abs(Ws)), 1.0)
            return (Wq, gamma)

        @jax.custom_vjp
        def absmean(W):
            return _absmean_core(W)[0]

        def _absmean_fwd(W):
            Wq, gamma = _absmean_core(W)
            return (Wq, gamma)

        def _absmean_bwd(gamma, g):
            return (g / gamma,)
        absmean.defvjp(_absmean_fwd, _absmean_bwd)

        def layernorm(x, w, b, eps=LN_EPS):
            mu = jnp.mean(x, axis=-1, keepdims=True)
            var = jnp.mean((x - mu) ** 2, axis=-1, keepdims=True)
            return (x - mu) * jax.lax.rsqrt(var + eps) * w + b
        key = jax.random.key(seed)
        k1, k2, k3 = jax.random.split(key, 3)
        d, h = (128, 512)
        B, T = (8, 256)
        return {'x': jax.random.normal(k1, (B, T, d), jnp.float32), 'W_fc': jax.random.normal(k2, (h, d), jnp.float32), 'ln_w': jnp.ones((h,), jnp.float32), 'ln_b': jnp.zeros((h,), jnp.float32), 'W_proj': jax.random.normal(k3, (d, h), jnp.float32)}
    _L0_ffn_in = _L0_ffn_setup()
    _d = {'L0_attn_x': _L0_attn_in['x'], 'L0_attn_wq': _L0_attn_in['wq'], 'L0_attn_bq': _L0_attn_in['bq'], 'L0_attn_wk': _L0_attn_in['wk'], 'L0_attn_bk': _L0_attn_in['bk'], 'L0_attn_wv': _L0_attn_in['wv'], 'L0_attn_bv': _L0_attn_in['bv'], 'L0_attn_wo': _L0_attn_in['wo'], 'L0_attn_bo': _L0_attn_in['bo'], 'L0_ffn_W_fc': _L0_ffn_in['W_fc'], 'L0_ffn_ln_w': _L0_ffn_in['ln_w'], 'L0_ffn_ln_b': _L0_ffn_in['ln_b'], 'L0_ffn_W_proj': _L0_ffn_in['W_proj']}
    _x0 = _d['L0_attn_x']
    _d['L0_attn_x'] = jax.random.normal(jax.random.fold_in(jax.random.key(seed), 1), (1, 2048, 128), dtype=_x0.dtype)
    del _x0
    return _d

def reference(L0_attn_x, L0_attn_wq, L0_attn_bq, L0_attn_wk, L0_attn_bk, L0_attn_wv, L0_attn_bv, L0_attn_wo, L0_attn_bo, L0_ffn_W_fc, L0_ffn_ln_w, L0_ffn_ln_b, L0_ffn_W_proj):

    def _L0_attn_ref(x, wq, bq, wk, bk, wv, bv, wo, bo):
        import jax, jax.numpy as jnp
        import numpy as np
        B, S, HID = (2, 256, 128)
        NH = 16
        HD = HID // NH
        BASE = 10000.0

        def rotate_half(x):
            x1, x2 = jnp.split(x, 2, axis=-1)
            return jnp.concatenate((-x2, x1), axis=-1)
        b, s, _ = x.shape

        def proj(w, bias):
            return (x @ w.T + bias).reshape(b, s, NH, HD).transpose(0, 2, 1, 3)
        q = proj(wq, bq)
        k = proj(wk, bk)
        v = proj(wv, bv)
        inv_freq = 1.0 / BASE ** (jnp.arange(0, HD, 2, dtype=jnp.float32) / HD)
        t = jnp.arange(s, dtype=jnp.float32)
        freqs = jnp.einsum('i,j->ij', t, inv_freq)
        emb = jnp.concatenate((freqs, freqs), axis=-1)
        cos = jnp.cos(emb)[None, None]
        sin = jnp.sin(emb)[None, None]
        q = q * cos + rotate_half(q) * sin
        k = k * cos + rotate_half(k) * sin
        scores = jnp.einsum('bhqd,bhkd->bhqk', q, k) / np.sqrt(HD).astype(np.float32)
        attn = jax.nn.softmax(scores, axis=-1)
        out = jnp.einsum('bhqk,bhkd->bhqd', attn, v)
        out = out.transpose(0, 2, 1, 3).reshape(b, s, HID)
        return out @ wo.T + bo

    def _L0_ffn_ref(x, W_fc, ln_w, ln_b, W_proj):
        import jax, jax.numpy as jnp
        import numpy as np
        EPS = 1e-06
        LN_EPS = 1e-05

        def _absmean_core(W):
            gamma = jnp.mean(jnp.abs(W)) + EPS
            Ws = W / gamma
            Wq = jnp.sign(Ws) * jnp.minimum(jnp.round(jnp.abs(Ws)), 1.0)
            return (Wq, gamma)

        @jax.custom_vjp
        def absmean(W):
            return _absmean_core(W)[0]

        def _absmean_fwd(W):
            Wq, gamma = _absmean_core(W)
            return (Wq, gamma)

        def _absmean_bwd(gamma, g):
            return (g / gamma,)
        absmean.defvjp(_absmean_fwd, _absmean_bwd)

        def layernorm(x, w, b, eps=LN_EPS):
            mu = jnp.mean(x, axis=-1, keepdims=True)
            var = jnp.mean((x - mu) ** 2, axis=-1, keepdims=True)
            return (x - mu) * jax.lax.rsqrt(var + eps) * w + b
        h = jnp.einsum('btd,hd->bth', x, absmean(W_fc))
        h = jax.nn.gelu(h, approximate=False)
        h = layernorm(h, ln_w, ln_b)
        return jnp.einsum('bth,dh->btd', h, absmean(W_proj))
    x = L0_attn_x
    x = x + 0.5 * _L0_ffn_ref(_layernorm(x, axis=-1), L0_ffn_W_fc, L0_ffn_ln_w, L0_ffn_ln_b, L0_ffn_W_proj)
    x = x + _L0_attn_ref(_layernorm(x, axis=-1), L0_attn_wq, L0_attn_bq, L0_attn_wk, L0_attn_bk, L0_attn_wv, L0_attn_bv, L0_attn_wo, L0_attn_bo)
    x = x + 0.5 * _L0_ffn_ref(_layernorm(x, axis=-1), L0_ffn_W_fc, L0_ffn_ln_w, L0_ffn_ln_b, L0_ffn_W_proj)
    return x

_drawn_inputs = setup_inputs


def setup_inputs(seed=0):
    import zlib

    import numpy as np

    out = dict(_drawn_inputs(seed))
    spreads = {'L0_attn_bq': (0.0, 0.8),
     'L0_attn_bk': (0.0, 0.8),
     'L0_attn_bv': (0.0, 0.8),
     'L0_attn_bo': (0.0, 0.8),
     'L0_ffn_ln_w': (1.0, 0.2),
     'L0_ffn_ln_b': (0.0, 0.1)}
    factors = {'L0_attn_wq': 8.0, 'L0_attn_wk': 8.0, 'L0_attn_wv': 3.562, 'L0_attn_wo': 3.195}
    for name, (base, spread) in spreads.items():
        noise = np.random.default_rng([zlib.crc32(name.encode()), seed]).standard_normal(out[name].shape)
        drawn = base * np.exp(spread * noise) if base else spread * noise
        out[name] = jnp.asarray(drawn.astype(out[name].dtype))
    for name, factor in factors.items():
        out[name] = (out[name] * factor).astype(out[name].dtype)
    return out
```

```python
from contextlib import ExitStack

import numpy as np

import concourse.bass as bass
from concourse import mybir

F32 = mybir.dt.float32
BF16 = mybir.dt.bfloat16
ALU = mybir.AluOpType
ACT = mybir.ActivationFunctionType
AX = mybir.AxisListType

P = 128
S = 2048
D = 128
H = 512
NH = 16
HD = D // NH
NT = S // P
CT = 4
NC = NT // CT
CS = CT * P
KH = H // P
LN_EPS = 1e-5
ABS_EPS = 1e-6

Q_PART = (0, 0, 1, 1, 2, 0)
K_PART = (0, 1, 0, 1, 0, 2)
HR = 64
R_QK = len(Q_PART) * HD
R_ALL = R_QK + 3

PAIRS = NH // 2
SCALE = float(1.0 / np.sqrt(np.float32(HD)))
VW = HD + 1
VCOLS = NH * VW + 32 - VW

A_STEP = 2 * CT * 2
B_STEP = 2 * NT
BATCH = 4
NB = B_STEP // BATCH
LEAD = 25
PRING = 16
PREP_AT, NORM_AT, ROWS_AT = 6, 8, 11
SEL_BATCH, MT_BATCH = 2, 5

A_IT = PAIRS * A_STEP
B_IT = PAIRS * B_STEP
PV_IT = PAIRS * NB

WARM = 20
SETUP_V = 8
W_DMAS = 11

C_TILE = CT
C_TWO = 2
C_ONE = 1
C_RING = PRING // BATCH


def rope_tables():
    inv = (1.0 / 10000.0 ** (np.arange(0, HD, 2, dtype=np.float32) / np.float32(HD))).astype(np.float32)
    ang = (np.arange(S, dtype=np.float32)[:, None] * inv[None, :]).astype(np.float32).astype(np.float64)
    cos = np.concatenate([np.cos(ang), np.cos(ang)], 1)
    sin = np.concatenate([-np.sin(ang), np.sin(ang)], 1)
    both = np.stack([cos, sin], 0).astype(np.float32)
    return np.ascontiguousarray(both.reshape(2, NT, P, HD).transpose(2, 0, 1, 3))


def macaron(nc, x, wq, bq, wk, bk, wv, bv, wo, bo, w_fc, ln_w, ln_b, w_proj, out):
    rope_dram = nc.inline_tensor(rope_tables(), name="rope_tables").ap()

    with ExitStack() as ctx:
        def sb(name, shape, dt=F32):
            return ctx.enter_context(nc.sbuf_tensor(name, shape, dt))

        def sem(name):
            return ctx.enter_context(nc.semaphore(name))

        ps = ctx.enter_context(nc.psum_tensor("ps", [P, 8, 512], F32))
        psb = ps[:, :, :].bitcast(BF16)
        FC, TR, PR, TP = 0, 4, 6, 7
        A0, B0, PO, MISC = 0, 4, 6, 7

        X = sb("X", [P, NT, D])
        X1 = sb("X1", [P, NT, D])
        X2 = sb("X2", [P, NT, D])
        AO = X
        Y = X1
        XB = sb("XB", [P, NT, D])
        ring = sb("ring", [P, PRING, CS])
        hid = ring[:, 0:CT, :]
        hn = ring[:, CT:2 * CT, :]
        hT = ring[:, 2 * CT:3 * CT, :].rearrange("p i (k n) -> p i k n", k=KH)
        XT = ring[:, 3 * CT, :]
        xn = sb("xn", [P, CT, D])
        st = sb("st", [P, CT, 6])
        mv = sb("mv", [P, CT, 2])
        ve = sb("ve", [P, CT])
        rs = sb("rs", [P, CT])
        sth = sb("sth", [P, CT, 6])
        mvh = sb("mvh", [P, CT, 2])
        veh = sb("veh", [P, CT])
        rsh = sb("rsh", [P, CT])
        eps = sb("eps", [P, CT])
        half_neg = sb("half_neg", [P, CT])
        ident = sb("ident", [P, P])
        identb = sb("identb", [P, P], BF16)
        ones = sb("ones", [P, P])
        wfc_n = sb("wfc_n", [P, KH, D])
        wpj_n = sb("wpj_n", [P, H])
        tern = sb("tern", [P, 2, H], BF16)
        below = sb("below", [P, 2, H], BF16)
        asum = sb("asum", [P, 2])
        gam = sb("gam", [P, 2])
        thr = sb("thr", [P, 2])
        nthr = sb("nthr", [P, 2])
        WfcT = sb("WfcT", [P, H])
        WpT = sb("WpT", [P, KH, D])
        WpS = sb("WpS", [P, KH, D])
        lnw = sb("lnw", [P, KH])
        lnb = sb("lnb", [P, KH])
        lnbB = sb("lnbB", [P, KH, P])
        halfb = sb("halfb", [P, D])
        w_n = sb("w_n", [P, 4, D])
        WT = sb("WT", [P, 4, D])
        biasB = sb("biasB", [P, 4, D])
        rope = sb("rope", [P, 2, NT, HD])
        qk = sb("qk", [P, 2, CT, D])
        qc = X[:, 0:2 * CT, :].rearrange("p (n t) d -> p n t d", n=2)
        qs = X[:, 2 * CT:4 * CT, :].rearrange("p (n t) d -> p n t d", n=2)
        part = sb("part", [P, 3, 2, CT, D], BF16)
        terms = sb("terms", [P, 2, CT, NH, HR], BF16)
        KT = sb("KT", [P, PAIRS, S], BF16)
        QT = sb("QT", [P, PAIRS, S], BF16)
        QS = sb("QS", [P, PAIRS, CS], BF16)
        Vx = sb("Vx", [P, NT, VCOLS])
        mh = sb("mh", [P, 2, A_STEP])
        nm = sb("nm", [P, 2, 2 * CT])
        nr = sb("nr", [P, 2, 2 * CT])
        mp = sb("mp", [P, 2, 2 * 3 * CT], BF16)
        mrow = sb("mrow", [2 * 3 * CT, 2, P], BF16)
        outT = sb("outT", [P, 2, CS])
        pick = sb("pick", [P, 2 * VW])
        rec = sb("rec", [P, 2, CT, 2, 1])

        x_in = sem("x_in")
        w_in = sem("w_in")
        wf_in = sem("wf_in")
        ident0 = sem("ident0")
        consts = sem("consts")
        setup_v = sem("setup_v")
        setup_p = sem("setup_p")
        ln_mv = sem("ln_mv")
        ln_ve = sem("ln_ve")
        ln_rs = sem("ln_rs")
        xn_ready = sem("xn_ready")
        xt_done = sem("xt_done")
        xt_ready = sem("xt_ready")
        fc_ready = sem("fc_ready")
        h_ready = sem("h_ready")
        h_mv = sem("h_mv")
        h_ve = sem("h_ve")
        h_rs = sem("h_rs")
        n_ready = sem("n_ready")
        nt_done = sem("nt_done")
        nt_ready = sem("nt_ready")
        pr_ready = sem("pr_ready")
        x1_ready = sem("x1_ready")
        xb_ready = sem("xb_ready")
        qkv_ready = sem("qkv_ready")
        qk_ev = sem("qk_ev")
        q_step = sem("q_step")
        parts_ready = sem("parts_ready")
        terms_k = sem("terms_k")
        terms_q = sem("terms_q")
        k_tr = sem("k_tr")
        q_tr = sem("q_tr")
        kt_ev = sem("kt_ev")
        qt_ev = sem("qt_ev")
        v_set = sem("v_set")
        q_in = [sem(f"q_in{j}") for j in range(PAIRS)]
        m_in = [sem(f"m_in{j}") for j in range(PAIRS)]
        a_ready = sem("a_ready")
        a_free = sem("a_free")
        b_ready = sem("b_ready")
        p_ready = sem("p_ready")
        pv_done = sem("pv_done")
        po_free = sem("po_free")
        sel_done = sem("sel_done")
        misc_free = sem("misc_free")
        m_step = sem("m_step")
        mp_ready = sem("mp_ready")
        rows_set = sem("rows_set")
        rows_ready = sem("rows_ready")
        rec_ready = sem("rec_ready")
        y_out = sem("y_out")

        block = ctx.enter_context(nc.Block())

        def chunk(t, c):
            return t[:, bass.ds(c * CT, CT), :]

        @block.sync
        def _(sp):
            sp.dma_start(X[:, :, :], x.rearrange("a (t p) d -> p (a t) d", p=P)).then_inc(x_in, 16)
            sp.dma_start(wfc_n[:, :, :], w_fc.rearrange("(k p) d -> p k d", p=P)).then_inc(wf_in, 16)
            sp.dma_start(wpj_n[:, :], w_proj).then_inc(wf_in, 16)
            sp.dma_start(lnw[:, :], ln_w.rearrange("(k p) -> p k", p=P), allow_slow_non_contiguous=True).then_inc(w_in, 16)
            sp.dma_start(lnb[:, :], ln_b.rearrange("(k p) -> p k", p=P), allow_slow_non_contiguous=True).then_inc(w_in, 16)
            for n, w in enumerate((wq, wk, wv, wo)):
                sp.dma_start(w_n[:, n, :], w).then_inc(w_in, 16)
            for n, b in enumerate((bq, bk, bv, bo)):
                sp.dma_start(biasB[:, n, :], b.partition_broadcast(P)).then_inc(w_in, 16)
            sp.dma_start(rope[:, :, :, :], rope_dram).then_inc(w_in, 16)

            def rows(i, c):
                j = i % PAIRS
                sp.wait_ge(rows_ready, c * PAIRS + i + 1)
                for h in range(2):
                    dst = QS[HR * h + R_QK:HR * h + R_ALL, j, :].rearrange("r (q n) -> r q n", q=CT)
                    sp.dma_start(dst, mrow[h * 3 * CT:(h + 1) * 3 * CT, i % 2, :]).then_inc(m_in[j], 16)

            rows(0, 0)
            with sp.Fori(0, NC - 1) as c:
                for i in range(1, PAIRS + 1):
                    rows(i, c)
            for i in range(1, PAIRS):
                rows(i, NC - 1)

            with sp.Fori(0, NC) as c:
                sp.wait_ge(x1_ready, c + 2 * NC + C_ONE + 1)
                sp.dma_start(out.rearrange("a (t p) d -> p (a t) d", p=P)[:, bass.ds(c * CT, CT), :],
                             chunk(Y, c)).then_inc(y_out, 16)
            sp.wait_ge(y_out, 16 * NC)

        @block.gpsimd
        def _(pool):
            g = nc.gpsimd
            for free, credit in ((xt_done, C_ONE), (xt_ready, C_ONE), (h_ready, C_TILE), (n_ready, C_TILE),
                                 (nt_done, C_TILE), (nt_ready, C_TWO), (x1_ready, C_ONE), (qk_ev, C_TILE),
                                 (terms_k, C_ONE), (terms_q, C_ONE), (k_tr, 4), (q_tr, 4), (kt_ev, C_TWO),
                                 (qt_ev, C_TWO), (p_ready, C_TWO), (pv_done, C_RING), (po_free, C_ONE),
                                 (sel_done, C_TWO), (misc_free, C_ONE)):
                pool.sem_inc(free, credit)
            g.memset(ident[:, :], 0.0)
            g.memset(identb[:, :], 0.0)
            g.memset(pick[:, :], 0.0).then_inc(ident0, 1)
            pool.wait_ge(ident0, 1)
            g.affine_select(out=ident[:, :], in_=ident[:, :], compare_op=ALU.not_equal, fill=1.0, base=0,
                            pattern=[[-1, P]], channel_multiplier=1)
            g.affine_select(out=identb[:, :], in_=identb[:, :], compare_op=ALU.not_equal, fill=1.0, base=0,
                            pattern=[[-1, P]], channel_multiplier=1)
            for par in range(2):
                g.affine_select(out=pick[:, :].rearrange("p (h n) -> p h n", h=2),
                                in_=pick[:, :].rearrange("p (h n) -> p h n", h=2),
                                compare_op=ALU.not_equal, fill=1.0, base=-32 * par,
                                pattern=[[-64, 2], [-1, VW]], channel_multiplier=1).then_inc(ident0, 1)
                pool.wait_ge(ident0, par + 2)
            g.memset(half_neg[:, :], -0.5)
            g.memset(eps[:, :], LN_EPS)
            g.memset(ones[:, :], 1.0).then_inc(consts, 1)
            g.memset(Vx[:, :, :], 0.0).then_inc(v_set, 1)
            pool.wait_ge(v_set, 1)
            g.memset(Vx[:, :, 0:NH * VW].rearrange("p t (h n) -> p t h n", n=VW)[:, :, :, HD:VW], 1.0)
            g.memset(terms[:, 0, :, :, R_QK:HR], 0.0)
            g.memset(terms[:, 1, :, :, R_QK:HR], 1.0).then_inc(v_set, 1)

            def ln_scale(which, c):
                n = c + NC * which + 1
                pool.wait_ge(ln_mv, n)
                g.tensor_tensor(ve[:, :], mv[:, :, 1], eps[:, :], ALU.add).then_inc(ln_ve, 1)
                pool.wait_ge(ln_ve, n)
                g.tensor_tensor(rs[:, :], ve[:, :], half_neg[:, :], ALU.pow).then_inc(ln_rs, 1)

            def ffn(p, c):
                src = (X, X2)[p]
                ln_scale(2 * p, c)
                g.tensor_tensor(chunk(XB, c), chunk(src, c),
                                halfb[:, :].unsqueeze(1).broadcast_to([P, CT, D]), ALU.add).then_inc(xb_ready, 1)
                for i in range(CT):
                    n = (c + p * NC) * CT + i + 1
                    pool.wait_ge(h_mv, n)
                    g.tensor_tensor(veh[:, i:i + 1], mvh[:, i, 1:2], eps[:, 0:1], ALU.add).then_inc(h_ve, 1)
                    pool.wait_ge(h_ve, n)
                    g.tensor_tensor(rsh[:, i:i + 1], veh[:, i:i + 1], half_neg[:, 0:1], ALU.pow).then_inc(h_rs, 1)

            pool.wait_ge(x_in, 16)
            pool.wait_ge(setup_v, SETUP_V)
            with pool.Fori(0, NC) as c:
                ffn(0, c)

            pool.wait_ge(w_in, 16 * W_DMAS)
            with pool.Fori(0, NC) as c:
                ln_scale(1, c)
                pool.wait_ge(parts_ready, c + 1)
                pool.wait_ge(q_tr, c * 4 + 4)
                g.tensor_tensor(chunk(X2, c), chunk(X1, c),
                                biasB[:, 3, :].unsqueeze(1).broadcast_to([P, CT, D]), ALU.add).then_inc(xb_ready, 1)
                tq = terms[:, 0, :, :, :].rearrange("p t h r -> p (t h) r")

                def pq(n):
                    return part[:, n, 0, :, :].rearrange("p t (h d) -> p (t h) d", d=HD)

                for r in range(len(Q_PART)):
                    last = g.tensor_copy(tq[:, :, r * HD:(r + 1) * HD], pq(Q_PART[r]))
                last.then_inc(terms_q, 1)

            def load_q(j, c):
                for h in range(2):
                    g.dma_start(QS[HR * h:HR * h + R_QK, j, :],
                                QT[HR * h:HR * h + R_QK, j, bass.ds(c * CS, CS)]).then_inc(q_in[j], 16)

            pool.wait_ge(qt_ev, 2 + 4 * NC)
            for j in range(PAIRS):
                load_q(j, 0)
            with pool.Fori(1, NC) as c:
                for j in range(PAIRS):
                    pool.wait_ge(b_ready, c * B_IT - B_IT + (j + 1) * B_STEP)
                    load_q(j, c)

            with pool.Fori(0, NC) as c:
                ffn(1, c)

        @block.vector
        def _(dve):
            v = nc.vector
            chain = [0]

            def link(ins):
                chain[0] += 1
                ins.then_inc(setup_v, 1)
                dve.wait_ge(setup_v, chain[0])

            dve.wait_ge(wf_in, 32)
            natural = (wfc_n[:, :, :].rearrange("p k d -> p (k d)"), wpj_n[:, :])
            v.tensor_reduce(asum[:, 0:1], natural[0], AX.X, ALU.add, apply_absolute_value=True)
            link(v.tensor_reduce(asum[:, 1:2], natural[1], AX.X, ALU.add, apply_absolute_value=True))
            dve.wait_ge(setup_p, 1)
            link(v.tensor_scalar(gam[:, :], ps[:, TP, 0:2], 1.0 / (H * D), ABS_EPS, ALU.mult, ALU.add))
            v.tensor_scalar(thr[:, :], gam[:, :], 0.5, None, ALU.mult)
            link(v.tensor_scalar(nthr[:, :], gam[:, :], -0.5, None, ALU.mult))
            for n in range(2):
                last = v.tensor_scalar(below[:, n, :], natural[n], nthr[:, n:n + 1], None, ALU.is_lt)
            link(last)
            for n in range(2):
                last = v.scalar_tensor_tensor(tern[:, n, :], natural[n], thr[:, n:n + 1], below[:, n, :],
                                              ALU.is_gt, ALU.subtract)
            link(last)
            dve.wait_ge(setup_p, 2)
            v.tensor_copy(WfcT[:, :], psb[:, TR, 0:H])
            link(v.tensor_copy(WpT[:, :, :], psb[:, TR + 1, 0:H].rearrange("p (k d) -> p k d", k=KH)))
            dve.wait_ge(w_in, 16 * W_DMAS)
            dve.wait_ge(consts, 1)
            for k in range(KH):
                v.tensor_scalar(WpS[:, k, :], WpT[:, k, :], lnw[:, k:k + 1], None, ALU.mult)
                last = v.tensor_scalar(lnbB[:, k, :], ones[:, :], lnb[:, k:k + 1], None, ALU.mult)
            link(last)
            dve.wait_ge(setup_p, 3)
            v.tensor_copy(WT[:, :, :], ps[:, TR, :].rearrange("p (n d) -> p n d", n=4))
            link(v.tensor_scalar(halfb[:, :], ps[:, PR, 0:D], 0.5, None, ALU.mult))
            assert chain[0] == SETUP_V, chain[0]

            def norm_rows(which, slot, src, c):
                n = c + NC * which + 1
                for i in range(CT):
                    v.bn_stats(st[:, i, :], src[:, bass.ds(c * CT + i, 1), :].rearrange("p t d -> p (t d)"))
                dve.drain()
                for i in range(CT):
                    last = v.bn_aggr(mv[:, i, :], st[:, i, :])
                last.then_inc(ln_mv, 1)
                dve.wait_ge(ln_rs, n)
                dve.wait_ge(xt_done, c + NC * slot + C_ONE)
                for i in range(CT):
                    last = v.tensor_scalar(xn[:, i, :], src[:, bass.ds(c * CT + i, 1), :].rearrange("p t d -> p (t d)"),
                                           mv[:, i, 0:1], rs[:, i:i + 1], ALU.subtract, ALU.mult)
                last.then_inc(xn_ready, 1)

            def ffn(p, c):
                src, dst = ((X, X1), (X2, Y))[p]
                norm_rows(2 * p, 3 * p, src, c)

                def stats(i):
                    n = (c + p * NC) * CT + i
                    dve.wait_ge(h_ready, n + 5)
                    v.bn_stats(sth[:, i, :], hid[:, i, :])
                    dve.drain()
                    v.bn_aggr(mvh[:, i, :], sth[:, i, :]).then_inc(h_mv, 1)

                def norm(i):
                    n = (c + p * NC) * CT + i
                    dve.wait_ge(h_rs, n + 1)
                    dve.wait_ge(nt_done, n + 1)
                    v.tensor_scalar(hn[:, i, :], hid[:, i, :], mvh[:, i, 0:1], rsh[:, i:i + 1],
                                    ALU.subtract, ALU.mult).then_inc(n_ready, 1)

                stats(0)
                for i in range(1, CT):
                    stats(i)
                    norm(i - 1)
                norm(CT - 1)
                dve.wait_ge(pr_ready, c + 2 * p * NC + 1)
                dve.wait_ge(xb_ready, c + 2 * p * NC + 1)
                v.scalar_tensor_tensor(chunk(dst, c), ps[:, PR, :].rearrange("p (t d) -> p t d", t=CT), 0.5,
                                       chunk(XB, c), ALU.mult, ALU.add).then_inc(x1_ready, 1)

            dve.wait_ge(x_in, 16)
            with dve.Fori(0, NC) as c:
                ffn(0, c)

            dve.wait_ge(v_set, 2)
            dve.wait_ge(x1_ready, NC + 1)
            QSTEPS = 5

            with dve.Fori(0, NC) as c:
                norm_rows(1, 1, X1, c)
                for i in range(CT):
                    dve.wait_ge(qkv_ready, c * CT + i + 1)
                    v.tensor_tensor(qk[:, :, i, :], ps[:, FC + i % 3, 0:2 * D].rearrange("p (n d) -> p n d", n=2),
                                    biasB[:, 0:2, :], ALU.add)
                    last = v.tensor_tensor(
                        Vx[:, bass.ds(c * CT + i, 1), 0:NH * VW].rearrange("p t (h n) -> p (t h) n", n=VW)[:, :, 0:HD],
                        ps[:, FC + i % 3, 2 * D:3 * D].rearrange("p (h n) -> p h n", n=HD),
                        biasB[:, 2, :].rearrange("p (h n) -> p h n", n=HD), ALU.add)
                    last.then_inc(qk_ev, 1)
                dve.wait_ge(qk_ev, c * CT + CT + 4)
                half = HD // 2
                for n in range(2):
                    x4 = qk[:, n, :, :].rearrange("p t (h d) -> p t h d", d=HD)
                    c4 = qc[:, n, :, :].rearrange("p t (h d) -> p t h d", d=HD)
                    s4 = qs[:, n, :, :].rearrange("p t (h d) -> p t h d", d=HD)
                    cos = rope[:, 0, bass.ds(c * CT, CT), :].unsqueeze(2)
                    sin = rope[:, 1, bass.ds(c * CT, CT), :].unsqueeze(2)
                    v.tensor_tensor(c4, x4, cos.broadcast_to([P, CT, NH, HD]), ALU.mult)
                    v.tensor_tensor(s4[:, :, :, 0:half], x4[:, :, :, half:HD],
                                    sin[:, :, :, 0:half].broadcast_to([P, CT, NH, half]), ALU.mult)
                    last = v.tensor_tensor(s4[:, :, :, half:HD], x4[:, :, :, 0:half],
                                           sin[:, :, :, half:HD].broadcast_to([P, CT, NH, half]), ALU.mult)
                steps = [0]

                def step(ins):
                    steps[0] += 1
                    ins.then_inc(q_step, 1)
                    dve.wait_ge(q_step, c * QSTEPS + steps[0])

                def flat(t):
                    return t.rearrange("p n t d -> p (n t d)")

                step(last)
                step(v.tensor_tensor(flat(qk[:, :, :, :]), flat(qc[:, :, :, :]), flat(qs[:, :, :, :]), ALU.add))
                dve.wait_ge(terms_k, c + 1)
                dve.wait_ge(terms_q, c + 1)
                step(v.tensor_copy(flat(part[:, 0, :, :, :]), flat(qk[:, :, :, :])))
                step(v.tensor_tensor(flat(qc[:, :, :, :]), flat(qk[:, :, :, :]), flat(part[:, 0, :, :, :]), ALU.subtract))
                step(v.tensor_copy(flat(part[:, 1, :, :, :]), flat(qc[:, :, :, :])))
                v.tensor_tensor(flat(part[:, 2, :, :, :]), flat(qc[:, :, :, :]), flat(part[:, 1, :, :, :]),
                                ALU.subtract).then_inc(parts_ready, 1)
                assert steps[0] == QSTEPS
                for e in range(4):
                    dve.wait_ge(q_tr, c * 4 + e + 5)
                    v.tensor_copy(QT[:, 2 * e:2 * e + 2, bass.ds(c * CS, CS)],
                                  psb[:, (PR, FC + 3)[e % 2], :].rearrange("p (j n) -> p j n", j=2)).then_inc(qt_ev, 1)

            def row_max(n, c):
                u = n % A_STEP
                h, q, half_ = u % 2, u // 4, u // 2 % 2
                dve.wait_ge(a_ready, c * A_IT + n + 1)
                at = (h * CT + q) * 2 + half_
                v.tensor_reduce(mh[:, n // A_STEP % 2, at:at + 1],
                                ps[:, A0 + 2 * (n % 2):A0 + 2 * (n % 2) + 2, :].rearrange("p a b -> p (a b)"),
                                AX.X, ALU.max).then_inc(a_free, 1)

            MSTEPS = 4

            def cut_max(i, c):
                b = i % 2
                done = [0]

                def step(ins):
                    done[0] += 1
                    ins.then_inc(m_step, 1)
                    dve.wait_ge(m_step, (c * PAIRS + i) * MSTEPS + done[0])

                parts = mp[:, b, :].rearrange("p (h r q) -> p h r q", h=2, r=3)
                m3 = nm[:, b, :].rearrange("p (h q) -> p h q", h=2)
                r3 = nr[:, b, :].rearrange("p (h q) -> p h q", h=2)
                dve.wait_ge(a_free, c * A_IT + (i + 1) * A_STEP)
                step(v.tensor_reduce(nm[:, b, :], mh[:, b, :].rearrange("p (m n) -> p m n", n=2), AX.X, ALU.max,
                                     negate=True))
                step(v.tensor_copy(parts[:, :, 0, :], m3))
                step(v.tensor_tensor(r3, m3, parts[:, :, 0, :], ALU.subtract))
                step(v.tensor_copy(parts[:, :, 1, :], r3))
                v.tensor_tensor(parts[:, :, 2, :], r3, parts[:, :, 1, :], ALU.subtract).then_inc(mp_ready, 1)
                assert done[0] == MSTEPS

            def take_rows(i, c):
                dve.wait_ge(rows_set, c * PAIRS + i + 1)
                v.tensor_copy(mrow[:, i % 2, :], psb[0:2 * 3 * CT, MISC, 0:P])\
                    .then_inc(rows_ready, 1)

            def normalise(i, c):
                dve.wait_ge(sel_done, c * PAIRS + i + C_TWO + 1)
                o = ps[:, MISC, 0:CT * 2 * VW].rearrange("p (q h n) -> p q h n", q=CT, h=2)
                v.reciprocal(rec[:, i % 2], o[:, :, :, HD:VW]).then_inc(rec_ready, 1)
                dve.wait_ge(rec_ready, c * PAIRS + i + 1)
                v.tensor_tensor(AO[:, bass.ds(c * CT, CT), i * 2 * HD:(i + 1) * 2 * HD]
                                .rearrange("p q (h d) -> p q h d", h=2),
                                o[:, :, :, 0:HD], rec[:, i % 2].broadcast_to([P, CT, 2, HD]), ALU.mult)\
                    .then_inc(misc_free, 1)

            def window(w, c, last):
                for pos in range(A_STEP):
                    n = w * A_STEP + LEAD + pos
                    if not last or n < A_IT:
                        row_max(n, c)
                    if pos == PREP_AT and (not last or w < PAIRS - 1):
                        cut_max(w + 1, c)
                    if pos == NORM_AT and w:
                        normalise(w - 1, c)
                    if pos == ROWS_AT and (not last or w < PAIRS - 1):
                        take_rows(w + 1, c)
                if w == PAIRS - 1:
                    normalise(w, c)

            for n in range(LEAD):
                row_max(n, 0)
                if n == A_STEP - 1:
                    cut_max(0, 0)
            take_rows(0, 0)
            with dve.Fori(0, NC - 1) as c:
                for w in range(PAIRS):
                    window(w, c, False)
            for w in range(PAIRS):
                window(w, NC - 1, True)

            dve.wait_ge(xb_ready, 2 * NC)
            with dve.Fori(0, NC) as c:
                dve.wait_ge(xt_done, c + NC * 2 + C_ONE)
                v.tensor_copy(xn[:, :, :], chunk(AO, c)).then_inc(xn_ready, 1)
                dve.wait_ge(pr_ready, c + NC + 1)
                v.tensor_tensor(chunk(X2, c), ps[:, PR, :].rearrange("p (t d) -> p t d", t=CT), chunk(X2, c),
                                ALU.add).then_inc(x1_ready, 1)
            dve.wait_ge(x1_ready, 2 * NC + C_ONE)
            with dve.Fori(0, NC) as c:
                ffn(1, c)

        @block.scalar
        def _(act):
            a = nc.scalar
            def take_xt(slot, c):
                act.wait_ge(xt_done, c + NC * slot + C_ONE + 1)
                a.copy(XT, ps[:, TP, :]).then_inc(xt_ready, 1)

            def ffn(p, c):
                take_xt(3 * p, c)

                def gelu(i):
                    n = (c + p * NC) * CT + i
                    act.wait_ge(fc_ready, n + 1)
                    act.wait_ge(n_ready, n + 1)
                    a.activation(hid[:, i, :], ps[:, FC + i, :], ACT.Gelu).then_inc(h_ready, 1)

                def take_ht(i):
                    n = (c + p * NC) * CT + i
                    act.wait_ge(nt_done, n + 5)
                    a.copy(hT[:, i, :, :], ps[:, TR + i % 2, :].rearrange("p (k n) -> p k n", k=KH))\
                        .then_inc(nt_ready, 1)

                for i in range(CT):
                    gelu(i)
                for i in range(CT):
                    take_ht(i)

            with act.Fori(0, NC) as c:
                ffn(0, c)

            act.wait_ge(v_set, 2)
            with act.Fori(0, NC) as c:
                take_xt(1, c)
                act.wait_ge(parts_ready, c + 1)
                act.wait_ge(k_tr, c * 4 + 4)
                tk = terms[:, 1, :, :, :].rearrange("p t h r -> p (t h) r")
                for r in range(len(K_PART)):
                    last = a.copy(tk[:, :, r * HD:(r + 1) * HD],
                                  part[:, K_PART[r], 1, :, :].rearrange("p t (h d) -> p (t h) d", d=HD))
                last.then_inc(terms_k, 1)
                for e in range(4):
                    act.wait_ge(k_tr, c * 4 + e + 5)
                    a.copy(KT[:, 2 * e:2 * e + 2, bass.ds(c * CS, CS)],
                           psb[:, TR + e % 2, :].rearrange("p (j n) -> p j n", j=2)).then_inc(kt_ev, 1)

            def exp_unit(k, c):
                act.wait_ge(b_ready, c * B_IT + k + 1)
                if k % BATCH == 0:
                    act.wait_ge(pv_done, c * PV_IT + k // BATCH + 1)
                a.activation(ring[:, k % PRING, :], ps[:, B0 + k % 2, :], ACT.Exp, scale=SCALE).then_inc(p_ready, 1)

            def take_out(i, c):
                act.wait_ge(pv_done, c * PV_IT + (i + 1) * NB + PRING // BATCH)
                act.wait_ge(sel_done, c * PAIRS + i + 1)
                a.copy(outT[:, i % 2, :], ps[:, PO, :]).then_inc(po_free, 1)

            with act.Fori(0, NC) as c:
                for w in range(PAIRS):
                    for k in range(B_STEP):
                        exp_unit(w * B_STEP + k, c)
                        if k == 5 and w:
                            take_out(w - 1, c)
                take_out(PAIRS - 1, c)

            with act.Fori(0, NC) as c:
                take_xt(2, c)
            with act.Fori(0, NC) as c:
                ffn(1, c)

        @block.tensor
        def _(pe):
            t = nc.tensor

            pe.wait_ge(consts, 1)
            pe.wait_ge(setup_v, 1)
            t.matmul(ps[:, TP, 0:2], ones[:, :], asum[:, :], start=True, stop=True).then_inc(setup_p, 1)
            pe.wait_ge(setup_v, 5)
            for n in range(2):
                for k in range(KH):
                    last = t.transpose(psb[:, TR + n, k * P:(k + 1) * P], tern[:, n, k * P:(k + 1) * P], identb[:, :])
            last.then_inc(setup_p, 1)
            pe.wait_ge(setup_v, 7)
            pe.wait_ge(w_in, 16 * W_DMAS)
            for n in range(4):
                t.transpose(ps[:, TR, n * P:(n + 1) * P], w_n[:, n, :], ident[:, :])
            for k in range(KH):
                last = t.matmul(ps[:, PR, 0:D], lnbB[:, k, :], WpT[:, k, :], start=(k == 0), stop=(k == KH - 1))
            last.then_inc(setup_p, 1)
            pe.wait_ge(setup_v, SETUP_V)

            def put_xt(slot, c):
                pe.wait_ge(xn_ready, c + NC * slot + 1)
                pe.wait_ge(xt_ready, c + NC * slot + C_ONE)
                for i in range(CT):
                    last = t.transpose(ps[:, TP, i * P:(i + 1) * P], xn[:, i, :], ident[:, :])
                last.then_inc(xt_done, 1)
                pe.wait_ge(xt_ready, c + NC * slot + C_ONE + 1)

            def ffn(p, c):
                put_xt(3 * p, c)
                for i in range(CT):
                    n = (c + p * NC) * CT + i
                    pe.wait_ge(h_ready, n + 1)
                    t.matmul(ps[:, FC + i, :], XT[:, i * P:(i + 1) * P], WfcT[:, :], start=True, stop=True)\
                        .then_inc(fc_ready, 1)

                def turn(i):
                    n = (c + p * NC) * CT + i
                    pe.wait_ge(n_ready, n + CT + 1)
                    pe.wait_ge(nt_ready, n + 1)
                    for k in range(KH):
                        last = t.transpose(ps[:, TR + i % 2, k * P:(k + 1) * P], hn[:, i, k * P:(k + 1) * P],
                                           ident[:, :])
                    last.then_inc(nt_done, 1)

                def project(i):
                    n = (c + p * NC) * CT + i
                    pe.wait_ge(nt_ready, n + C_TWO + 1)
                    if i == 0:
                        pe.wait_ge(x1_ready, c + 2 * p * NC + C_ONE)
                    for k in range(KH):
                        last = t.matmul(ps[:, PR, i * D:(i + 1) * D], hT[:, i, k, :], WpS[:, k, :],
                                        start=(k == 0), stop=(k == KH - 1))
                    return last

                turn(0)
                for i in range(1, CT):
                    turn(i)
                    project(i - 1)
                project(CT - 1).then_inc(pr_ready, 1)

            with pe.Fori(0, NC) as c:
                ffn(0, c)

            pe.wait_ge(h_ready, NT + C_TILE)
            pe.wait_ge(nt_ready, NT + C_TWO)
            pe.wait_ge(x1_ready, NC + C_ONE)
            with pe.Fori(0, NC) as c:
                put_xt(1, c)
                for i in range(CT):
                    pe.wait_ge(qk_ev, c * CT + (CT if i < 3 else 1 + CT))
                    t.matmul(ps[:, FC + i % 3, 0:3 * D], XT[:, i * P:(i + 1) * P],
                             WT[:, 0:3, :].rearrange("p n d -> p (n d)"), start=True, stop=True).then_inc(qkv_ready, 1)
                for n, banks, ready, free, done in ((1, (TR, TR + 1), terms_k, kt_ev, k_tr),
                                                    (0, (PR, FC + 3), terms_q, qt_ev, q_tr)):
                    pe.wait_ge(ready, c + C_ONE + 1)
                    for e in range(4):
                        pe.wait_ge(free, c * 4 + e + 1)
                        for j in range(2):
                            for i in range(CT):
                                last = t.transpose(psb[:, banks[e % 2], (j * CT + i) * P:(j * CT + i + 1) * P],
                                                   terms[:, n, i, 4 * e + 2 * j:4 * e + 2 * j + 2, :]
                                                   .rearrange("p h r -> p (h r)"), identb[:, :])
                        last.then_inc(done, 1)

            pe.wait_ge(qk_ev, NT + C_TILE)
            for m in range(WARM):
                t.matmul(ps[:, FC + m % 3, :], identb[:, :], tern[:, 0, :], start=True, stop=True)
            pe.wait_ge(kt_ev, 4 * NC + C_TWO)
            pe.wait_ge(qt_ev, 4 * NC + C_TWO)
            pe.wait_ge(xt_ready, 2 * NC + C_ONE)

            def max_mm(m, c):
                n, x = m // 2, m % 2
                i, u = n // A_STEP, n % A_STEP
                j = i % PAIRS
                h, q, half = u % 2, u // 4, u // 2 % 2
                if x == 0:
                    if u == 0:
                        pe.wait_ge(q_in[j], (c + i // PAIRS + 1) * 32)
                    if type(c) is not int or n >= 2:
                        pe.wait_ge(a_free, c * A_IT + n - 1)
                r = slice(HR * h, HR * h + R_QK)
                mm = t.matmul(ps[:, A0 + 2 * (n % 2) + x, :], QS[r, j, q * P:(q + 1) * P],
                              KT[r, j, (2 * half + x) * 512:(2 * half + x + 1) * 512], start=True, stop=True)
                if x:
                    mm.then_inc(a_ready, 1)

            def exp_mm(i, k, c):
                b, r4 = k // BATCH, k % BATCH
                h, kt = r4 // 2, 2 * b + r4 % 2
                if k == 0:
                    pe.wait_ge(m_in[i], (c + 1) * 32)
                pe.wait_ge(p_ready, c * B_IT + i * B_STEP + k + 1)
                r = slice(HR * h, HR * h + R_ALL)
                t.matmul(ps[:, B0 + k % 2, :], KT[r, i, kt * P:(kt + 1) * P], QS[r, i, :],
                         start=True, stop=True).then_inc(b_ready, 1)

            def pv_batch(i, b, c):
                if b == 0:
                    pe.wait_ge(po_free, c * PAIRS + i + C_ONE)
                pe.wait_ge(p_ready, c * B_IT + i * B_STEP + (b + 1) * BATCH + C_TWO)
                for r4 in range(BATCH):
                    h, kt = r4 // 2, 2 * b + r4 % 2
                    col = (2 * i + h) * VW
                    mm = t.matmul(ps[32 * r4:32 * r4 + 32, PO, :], Vx[:, kt, col:col + 32],
                                  ring[:, (b * BATCH + r4) % PRING, :], start=(b == 0), stop=(b == NB - 1))
                mm.then_inc(pv_done, 1)

            def select(i, c, rows):
                pe.wait_ge(po_free, c * PAIRS + i + C_ONE + 1)
                pe.wait_ge(rows_ready, c * PAIRS + rows)
                pe.wait_ge(misc_free, c * PAIRS + i + C_ONE)
                for q in range(CT):
                    mm = t.matmul(ps[:, MISC, q * 2 * VW:(q + 1) * 2 * VW], outT[:, i % 2, q * P:(q + 1) * P],
                                  pick[:, :], start=True, stop=True)
                mm.then_inc(sel_done, 1)

            def turn_max(i, c):
                pe.wait_ge(mp_ready, c * PAIRS + i + 1)
                n = 2 * 3 * CT
                return t.transpose(psb[0:n, MISC, 0:P], mp[:, i % 2, :], identb[:, :])

            for m in range(2 * LEAD):
                max_mm(m, 0)
            turn_max(0, 0).then_inc(rows_set, 1)

            def steps(c, last):
                for i in range(PAIRS):
                    for k in range(B_STEP):
                        exp_mm(i, k, c)
                        m = i * B_STEP + k + 2 * LEAD
                        if not last or m < 2 * A_IT:
                            max_mm(m, c)
                        if k % BATCH == BATCH - 1:
                            b = k // BATCH
                            if b:
                                pv_batch(i, b - 1, c)
                            elif i:
                                pv_batch(i - 1, NB - 1, c)
                            if b == SEL_BATCH and i:
                                select(i - 1, c, i + 1)
                            if b == MT_BATCH and (not last or i < PAIRS - 1):
                                pe.wait_ge(misc_free, c * PAIRS + i + C_ONE)
                                turn_max(i + 1, c).then_inc(rows_set, 1)
                pv_batch(PAIRS - 1, NB - 1, c)
                select(PAIRS - 1, c, PAIRS + (0 if last else 1))

            with pe.Fori(0, NC - 1) as c:
                steps(c, False)
            steps(NC - 1, True)

            pe.wait_ge(misc_free, NC * PAIRS + C_ONE)
            with pe.Fori(0, NC) as c:
                put_xt(2, c)
                pe.wait_ge(x1_ready, c + NC + C_ONE)
                for i in range(CT):
                    last = t.matmul(ps[:, PR, i * D:(i + 1) * D], XT[:, i * P:(i + 1) * P], WT[:, 3, :],
                                    start=True, stop=True)
                last.then_inc(pr_ready, 1)
            with pe.Fori(0, NC) as c:
                ffn(1, c)


_INS = ['L0_attn_x', 'L0_attn_wq', 'L0_attn_bq', 'L0_attn_wk', 'L0_attn_bk', 'L0_attn_wv', 'L0_attn_bv',
        'L0_attn_wo', 'L0_attn_bo', 'L0_ffn_W_fc', 'L0_ffn_ln_w', 'L0_ffn_ln_b', 'L0_ffn_W_proj']
_OUTS = [((1, S, D), 'float32')]


def kernel(**inputs):
    import numpy as _np
    import concourse.bacc as _bacc
    from concourse import mybir as _mybir
    from concourse.bass_utils import run_bass_kernel_spmd as _run

    nc = _bacc.Bacc("TRN2", target_bir_lowering=False, num_devices=1)
    arrays, args = {}, []
    for name in _INS:
        a = _np.ascontiguousarray(inputs[name])
        arrays[f"in_{name}_dram"] = a
        args.append(nc.dram_tensor(f"in_{name}_dram", a.shape, _mybir.dt.from_np(a.dtype), kind="ExternalInput").ap())
    for i, (shape, dtype) in enumerate(_OUTS):
        dt = _mybir.dt.from_np(_np.dtype(dtype))
        args.append(nc.dram_tensor(f"out_{i}_dram", shape, dt, kind="ExternalOutput").ap())
    macaron(nc, *args)
    r = _run(nc, [arrays], core_ids=[0])
    return r.results[0]["out_0_dram"]
```

```python
from contextlib import ExitStack

import numpy as np

import concourse.bass as bass
from concourse import mybir

F32 = mybir.dt.float32
BF16 = mybir.dt.bfloat16
ALU = mybir.AluOpType
ACT = mybir.ActivationFunctionType
AX = mybir.AxisListType

P = 128
S = 2048
D = 128
H = 512
NH = 16
HD = D // NH
NT = S // P
CT = 4
NC = NT // CT
CS = CT * P
KH = H // P
LN_EPS = 1e-5
ABS_EPS = 1e-6

Q_PART = (0, 0, 1, 1, 2, 0)
K_PART = (0, 1, 0, 1, 0, 2)
HR = 64
R_QK = len(Q_PART) * HD
R_ALL = R_QK + 3

PAIRS = NH // 2
SCALE = float(1.0 / np.sqrt(np.float32(HD)))
VW = HD + 1
VCOLS = NH * VW + 32 - VW

A_STEP = 2 * CT * 2
B_STEP = 2 * NT
BATCH = 4
NB = B_STEP // BATCH
LEAD = 25
PRING = 16
PREP_AT, NORM_AT, ROWS_AT = 6, 8, 11
SEL_BATCH, MT_BATCH = 2, 5

A_IT = PAIRS * A_STEP
B_IT = PAIRS * B_STEP
PV_IT = PAIRS * NB

WARM = 20
SETUP_V = 8
W_DMAS = 11

C_TILE = CT
C_TWO = 2
C_ONE = 1
C_RING = PRING // BATCH


def rope_tables():
    inv = (1.0 / 10000.0 ** (np.arange(0, HD, 2, dtype=np.float32) / np.float32(HD))).astype(np.float32)
    ang = (np.arange(S, dtype=np.float32)[:, None] * inv[None, :]).astype(np.float32).astype(np.float64)
    cos = np.concatenate([np.cos(ang), np.cos(ang)], 1)
    sin = np.concatenate([-np.sin(ang), np.sin(ang)], 1)
    both = np.stack([cos, sin], 0).astype(np.float32)
    return np.ascontiguousarray(both.reshape(2, NT, P, HD).transpose(2, 0, 1, 3))


def macaron(nc, x, wq, bq, wk, bk, wv, bv, wo, bo, w_fc, ln_w, ln_b, w_proj, out):
    rope_dram = nc.inline_tensor(rope_tables(), name="rope_tables").ap()

    with ExitStack() as ctx:
        def sb(name, shape, dt=F32):
            return ctx.enter_context(nc.sbuf_tensor(name, shape, dt))

        def sem(name):
            return ctx.enter_context(nc.semaphore(name))

        ps = ctx.enter_context(nc.psum_tensor("ps", [P, 8, 512], F32))
        psb = ps[:, :, :].bitcast(BF16)
        FC, TR, PR, TP = 0, 4, 6, 7
        A0, B0, PO, MISC = 0, 4, 6, 7

        X = sb("X", [P, NT, D])
        X1 = sb("X1", [P, NT, D])
        X2 = sb("X2", [P, NT, D])
        AO = X
        Y = X1
        XB = sb("XB", [P, NT, D])
        ring = sb("ring", [P, PRING, CS])
        hid = ring[:, 0:CT, :]
        hn = ring[:, CT:2 * CT, :]
        hT = ring[:, 2 * CT:3 * CT, :].rearrange("p i (k n) -> p i k n", k=KH)
        XT = ring[:, 3 * CT, :]
        xn = sb("xn", [P, CT, D])
        st = sb("st", [P, CT, 6])
        mv = sb("mv", [P, CT, 2])
        ve = sb("ve", [P, CT])
        rs = sb("rs", [P, CT])
        sth = sb("sth", [P, CT, 6])
        mvh = sb("mvh", [P, CT, 2])
        veh = sb("veh", [P, CT])
        rsh = sb("rsh", [P, CT])
        eps = sb("eps", [P, CT])
        half_neg = sb("half_neg", [P, CT])
        ident = sb("ident", [P, P])
        identb = sb("identb", [P, P], BF16)
        ones = sb("ones", [P, P])
        wfc_n = sb("wfc_n", [P, KH, D])
        wpj_n = sb("wpj_n", [P, H])
        tern = sb("tern", [P, 2, H], BF16)
        below = sb("below", [P, 2, H], BF16)
        asum = sb("asum", [P, 2])
        gam = sb("gam", [P, 2])
        thr = sb("thr", [P, 2])
        nthr = sb("nthr", [P, 2])
        WfcT = sb("WfcT", [P, H])
        WpT = sb("WpT", [P, KH, D])
        WpS = sb("WpS", [P, KH, D])
        lnw = sb("lnw", [P, KH])
        lnb = sb("lnb", [P, KH])
        lnbB = sb("lnbB", [P, KH, P])
        halfb = sb("halfb", [P, D])
        w_n = sb("w_n", [P, 4, D])
        WT = sb("WT", [P, 4, D])
        biasB = sb("biasB", [P, 4, D])
        rope = sb("rope", [P, 2, NT, HD])
        qk = ring[:, 4:6, :].rearrange("p n (t d) -> p n t d", t=CT)
        qc = X[:, 0:2 * CT, :].rearrange("p (n t) d -> p n t d", n=2)
        qs = X[:, 2 * CT:4 * CT, :].rearrange("p (n t) d -> p n t d", n=2)
        part = ring[:, 0:3, :].rearrange("p a b -> p (a b)").bitcast(BF16)\
            .rearrange("p (r n t d) -> p r n t d", r=3, n=2, t=CT)
        terms = sb("terms", [P, 2, CT, NH, HR], BF16)
        KT = sb("KT", [P, PAIRS, S], BF16)
        QT = sb("QT", [P, PAIRS, S], BF16)
        QS = sb("QS", [P, 2, PAIRS, CS], BF16)
        Vx = sb("Vx", [P, NT, VCOLS])
        mh = sb("mh", [P, 2, A_STEP])
        nm = sb("nm", [P, 2, 2 * CT])
        nr = sb("nr", [P, 2, 2 * CT])
        mp = sb("mp", [P, 2, 2 * 3 * CT], BF16)
        mrow = sb("mrow", [2 * 3 * CT, 2, P], BF16)
        outT = sb("outT", [P, 2, CS])
        pick = sb("pick", [P, 2 * VW])
        rec = sb("rec", [P, 2, CT, 2, 1])

        x_in = sem("x_in")
        w_in = sem("w_in")
        wf_in = sem("wf_in")
        ident0 = sem("ident0")
        consts = sem("consts")
        setup_v = sem("setup_v")
        setup_p = sem("setup_p")
        ln_mv = sem("ln_mv")
        ln_ve = sem("ln_ve")
        ln_rs = sem("ln_rs")
        xn_ready = sem("xn_ready")
        xt_done = sem("xt_done")
        xt_ready = sem("xt_ready")
        fc_ready = sem("fc_ready")
        h_ready = sem("h_ready")
        h_mv = sem("h_mv")
        h_ve = sem("h_ve")
        h_rs = sem("h_rs")
        n_ready = sem("n_ready")
        nt_done = sem("nt_done")
        nt_ready = sem("nt_ready")
        pr_ready = sem("pr_ready")
        x1_ready = sem("x1_ready")
        xb_ready = sem("xb_ready")
        qkv_ready = sem("qkv_ready")
        qk_ev = sem("qk_ev")
        q_step = sem("q_step")
        parts_ready = sem("parts_ready")
        terms_k = sem("terms_k")
        terms_q = sem("terms_q")
        k_tr = sem("k_tr")
        q_tr = sem("q_tr")
        kt_ev = sem("kt_ev")
        qt_ev = sem("qt_ev")
        v_set = sem("v_set")
        q_in = [sem(f"q_in{j}") for j in range(PAIRS)]
        m_in = [sem(f"m_in{j}") for j in range(PAIRS)]
        a_ready = sem("a_ready")
        a_free = sem("a_free")
        b_ready = sem("b_ready")
        p_ready = sem("p_ready")
        pv_done = sem("pv_done")
        po_free = sem("po_free")
        sel_done = sem("sel_done")
        misc_free = sem("misc_free")
        m_step = sem("m_step")
        mp_ready = sem("mp_ready")
        rows_set = sem("rows_set")
        rows_ready = sem("rows_ready")
        rec_ready = sem("rec_ready")
        y_out = sem("y_out")

        block = ctx.enter_context(nc.Block())

        def chunk(t, c):
            return t[:, bass.ds(c * CT, CT), :]

        @block.sync
        def _(sp):
            sp.dma_start(X[:, :, :], x.rearrange("a (t p) d -> p (a t) d", p=P)).then_inc(x_in, 16)
            sp.dma_start(wfc_n[:, :, :], w_fc.rearrange("(k p) d -> p k d", p=P)).then_inc(wf_in, 16)
            sp.dma_start(wpj_n[:, :], w_proj).then_inc(wf_in, 16)
            sp.dma_start(lnw[:, :], ln_w.rearrange("(k p) -> p k", p=P), allow_slow_non_contiguous=True).then_inc(w_in, 16)
            sp.dma_start(lnb[:, :], ln_b.rearrange("(k p) -> p k", p=P), allow_slow_non_contiguous=True).then_inc(w_in, 16)
            for n, w in enumerate((wq, wk, wv, wo)):
                sp.dma_start(w_n[:, n, :], w).then_inc(w_in, 16)
            for n, b in enumerate((bq, bk, bv, bo)):
                sp.dma_start(biasB[:, n, :], b.partition_broadcast(P)).then_inc(w_in, 16)
            sp.dma_start(rope[:, :, :, :], rope_dram).then_inc(w_in, 16)

            def rows(i, c):
                j = i % PAIRS
                sp.wait_ge(rows_ready, c * PAIRS + i + 1)
                for h in range(2):
                    dst = QS[HR * h + R_QK:HR * h + R_ALL, h, j, :].rearrange("r (q n) -> r q n", q=CT)
                    sp.dma_start(dst, mrow[h * 3 * CT:(h + 1) * 3 * CT, i % 2, :]).then_inc(m_in[j], 16)

            rows(0, 0)
            with sp.Fori(0, NC - 1) as c:
                for i in range(1, PAIRS + 1):
                    rows(i, c)
            for i in range(1, PAIRS):
                rows(i, NC - 1)

            with sp.Fori(0, NC) as c:
                sp.wait_ge(x1_ready, c + 2 * NC + C_ONE + 1)
                sp.dma_start(out.rearrange("a (t p) d -> p (a t) d", p=P)[:, bass.ds(c * CT, CT), :],
                             chunk(Y, c)).then_inc(y_out, 16)
            sp.wait_ge(y_out, 16 * NC)

        @block.gpsimd
        def _(pool):
            g = nc.gpsimd
            for free, credit in ((xt_done, C_ONE), (xt_ready, C_ONE), (h_ready, C_TILE), (n_ready, C_TILE),
                                 (nt_done, C_TILE), (nt_ready, C_TWO), (x1_ready, C_ONE), (qk_ev, C_TILE),
                                 (terms_k, C_ONE), (terms_q, C_ONE), (k_tr, 4), (q_tr, 4), (kt_ev, C_TWO),
                                 (qt_ev, C_TWO), (p_ready, C_TWO), (pv_done, C_RING), (po_free, C_ONE),
                                 (sel_done, C_TWO), (misc_free, C_ONE)):
                pool.sem_inc(free, credit)
            g.memset(ident[:, :], 0.0)
            g.memset(identb[:, :], 0.0)
            g.memset(pick[:, :], 0.0).then_inc(ident0, 1)
            pool.wait_ge(ident0, 1)
            g.affine_select(out=ident[:, :], in_=ident[:, :], compare_op=ALU.not_equal, fill=1.0, base=0,
                            pattern=[[-1, P]], channel_multiplier=1)
            g.affine_select(out=identb[:, :], in_=identb[:, :], compare_op=ALU.not_equal, fill=1.0, base=0,
                            pattern=[[-1, P]], channel_multiplier=1)
            for par in range(2):
                g.affine_select(out=pick[:, :].rearrange("p (h n) -> p h n", h=2),
                                in_=pick[:, :].rearrange("p (h n) -> p h n", h=2),
                                compare_op=ALU.not_equal, fill=1.0, base=-32 * par,
                                pattern=[[-64, 2], [-1, VW]], channel_multiplier=1).then_inc(ident0, 1)
                pool.wait_ge(ident0, par + 2)
            g.memset(half_neg[:, :], -0.5)
            g.memset(eps[:, :], LN_EPS)
            g.memset(ones[:, :], 1.0).then_inc(consts, 1)
            g.memset(Vx[:, :, :], 0.0).then_inc(v_set, 1)
            pool.wait_ge(v_set, 1)
            g.memset(Vx[:, :, 0:NH * VW].rearrange("p t (h n) -> p t h n", n=VW)[:, :, :, HD:VW], 1.0)
            g.memset(QS[:, :, :, :], 0.0)
            g.memset(terms[:, 0, :, :, R_QK:HR], 0.0)
            g.memset(terms[:, 1, :, :, R_QK:HR], 1.0).then_inc(v_set, 1)

            def ln_scale(which, c):
                n = c + NC * which + 1
                pool.wait_ge(ln_mv, n)
                g.tensor_tensor(ve[:, :], mv[:, :, 1], eps[:, :], ALU.add).then_inc(ln_ve, 1)
                pool.wait_ge(ln_ve, n)
                g.tensor_tensor(rs[:, :], ve[:, :], half_neg[:, :], ALU.pow).then_inc(ln_rs, 1)

            def residual(p, c):
                g.tensor_tensor(chunk(XB, c), chunk((X, X2)[p], c),
                                halfb[:, :].unsqueeze(1).broadcast_to([P, CT, D]), ALU.add).then_inc(xb_ready, 1)

            def ffn_chunk(p, c, more):
                if more:
                    ln_scale(2 * p, c + 1)
                for i in range(CT):
                    n = (c + p * NC) * CT + i + 1
                    pool.wait_ge(h_mv, n)
                    g.tensor_tensor(veh[:, i:i + 1], mvh[:, i, 1:2], eps[:, 0:1], ALU.add).then_inc(h_ve, 1)
                    pool.wait_ge(h_ve, n)
                    g.tensor_tensor(rsh[:, i:i + 1], veh[:, i:i + 1], half_neg[:, 0:1], ALU.pow).then_inc(h_rs, 1)
                    if i == 0:
                        residual(p, c)

            def ffn(p):
                ln_scale(2 * p, 0)
                with pool.Fori(0, NC - 1) as c:
                    ffn_chunk(p, c, True)
                ffn_chunk(p, NC - 1, False)

            pool.wait_ge(x_in, 16)
            pool.wait_ge(setup_v, SETUP_V)
            ffn(0)

            pool.wait_ge(w_in, 16 * W_DMAS)
            with pool.Fori(0, NC) as c:
                ln_scale(1, c)
                g.tensor_tensor(chunk(X2, c), chunk(X1, c),
                                biasB[:, 3, :].unsqueeze(1).broadcast_to([P, CT, D]), ALU.add).then_inc(xb_ready, 1)

            def load_q(j, c):
                for h in range(2):
                    g.dma_start(QS[HR * h:HR * h + R_ALL, h, j, :],
                                QT[HR * h:HR * h + R_ALL, j, bass.ds(c * CS, CS)]).then_inc(q_in[j], 16)

            pool.wait_ge(qt_ev, 2 + 4 * NC)
            for j in range(PAIRS):
                load_q(j, 0)
            with pool.Fori(1, NC) as c:
                for j in range(PAIRS):
                    pool.wait_ge(b_ready, c * B_IT - B_IT + (j + 1) * B_STEP)
                    load_q(j, c)

            ffn(1)

        @block.vector
        def _(dve):
            v = nc.vector
            chain = [0]

            def link(ins):
                chain[0] += 1
                ins.then_inc(setup_v, 1)
                dve.wait_ge(setup_v, chain[0])

            dve.wait_ge(wf_in, 32)
            natural = (wfc_n[:, :, :].rearrange("p k d -> p (k d)"), wpj_n[:, :])
            v.tensor_reduce(asum[:, 0:1], natural[0], AX.X, ALU.add, apply_absolute_value=True)
            link(v.tensor_reduce(asum[:, 1:2], natural[1], AX.X, ALU.add, apply_absolute_value=True))
            dve.wait_ge(setup_p, 1)
            link(v.tensor_scalar(gam[:, :], ps[:, TP, 0:2], 1.0 / (H * D), ABS_EPS, ALU.mult, ALU.add))
            v.tensor_scalar(thr[:, :], gam[:, :], 0.5, None, ALU.mult)
            link(v.tensor_scalar(nthr[:, :], gam[:, :], -0.5, None, ALU.mult))
            for n in range(2):
                last = v.tensor_scalar(below[:, n, :], natural[n], nthr[:, n:n + 1], None, ALU.is_lt)
            link(last)
            for n in range(2):
                last = v.scalar_tensor_tensor(tern[:, n, :], natural[n], thr[:, n:n + 1], below[:, n, :],
                                              ALU.is_gt, ALU.subtract)
            link(last)
            dve.wait_ge(setup_p, 2)
            v.tensor_copy(WfcT[:, :], psb[:, TR, 0:H])
            link(v.tensor_copy(WpT[:, :, :], psb[:, TR + 1, 0:H].rearrange("p (k d) -> p k d", k=KH)))
            dve.wait_ge(w_in, 16 * W_DMAS)
            dve.wait_ge(consts, 1)
            for k in range(KH):
                v.tensor_scalar(WpS[:, k, :], WpT[:, k, :], lnw[:, k:k + 1], None, ALU.mult)
                last = v.tensor_scalar(lnbB[:, k, :], ones[:, :], lnb[:, k:k + 1], None, ALU.mult)
            link(last)
            dve.wait_ge(setup_p, 3)
            v.tensor_copy(WT[:, :, :], ps[:, TR, :].rearrange("p (n d) -> p n d", n=4))
            link(v.tensor_scalar(halfb[:, :], ps[:, PR, 0:D], 0.5, None, ALU.mult))
            assert chain[0] == SETUP_V, chain[0]

            def rows_of(src, c, i):
                return src[:, bass.ds(c * CT + i, 1), :].rearrange("p t d -> p (t d)")

            def row_stats(src, c):
                for i in range(CT):
                    v.bn_stats(st[:, i, :], rows_of(src, c, i))
                dve.drain()
                for i in range(CT):
                    last = v.bn_aggr(mv[:, i, :], st[:, i, :])
                last.then_inc(ln_mv, 1)

            def norm_rows(which, slot, src, c):
                dve.wait_ge(ln_rs, c + NC * which + 1)
                dve.wait_ge(xt_done, c + NC * slot + C_ONE)
                for i in range(CT):
                    last = v.tensor_scalar(xn[:, i, :], rows_of(src, c, i), mv[:, i, 0:1], rs[:, i:i + 1],
                                           ALU.subtract, ALU.mult)
                last.then_inc(xn_ready, 1)

            def hidden_stats(p, c, i):
                n = (c + p * NC) * CT + i
                dve.wait_ge(h_ready, n + CT + 1)
                v.bn_stats(sth[:, i, :], hid[:, i, :])
                dve.drain()
                v.bn_aggr(mvh[:, i, :], sth[:, i, :]).then_inc(h_mv, 1)

            def hidden_norm(p, c, i):
                n = (c + p * NC) * CT + i
                dve.wait_ge(h_rs, n + 1)
                dve.wait_ge(nt_done, n + 1)
                v.tensor_scalar(hn[:, i, :], hid[:, i, :], mvh[:, i, 0:1], rsh[:, i:i + 1],
                                ALU.subtract, ALU.mult).then_inc(n_ready, 1)

            def ffn_first(p, c):
                src = (X, X2)[p]
                row_stats(src, c)
                norm_rows(2 * p, 3 * p, src, c)

            def ffn_second(p, c, more):
                src, dst = ((X, X1), (X2, Y))[p]
                if more:
                    row_stats(src, c + 1)
                hidden_stats(p, c, 0)
                if more:
                    norm_rows(2 * p, 3 * p, src, c + 1)
                for i in range(1, CT):
                    hidden_stats(p, c, i)
                    hidden_norm(p, c, i - 1)
                hidden_norm(p, c, CT - 1)
                dve.wait_ge(pr_ready, c + 2 * p * NC + 1)
                dve.wait_ge(xb_ready, c + 2 * p * NC + 1)
                v.scalar_tensor_tensor(chunk(dst, c), ps[:, PR, :].rearrange("p (t d) -> p t d", t=CT), 0.5,
                                       chunk(XB, c), ALU.mult, ALU.add).then_inc(x1_ready, 1)

            def ffn(p):
                ffn_first(p, 0)
                with dve.Fori(0, NC - 1) as c:
                    ffn_second(p, c, True)
                ffn_second(p, NC - 1, False)

            dve.wait_ge(x_in, 16)
            ffn(0)

            dve.wait_ge(v_set, 2)
            dve.wait_ge(x1_ready, NC + 1)
            QSTEPS = 5

            def project_chunk(c, more):
                if more:
                    row_stats(X1, c + 1)
                for i in range(CT):
                    dve.wait_ge(qkv_ready, c * CT + i + 1)
                    v.tensor_tensor(qk[:, :, i, :], ps[:, FC + i % 3, 0:2 * D].rearrange("p (n d) -> p n d", n=2),
                                    biasB[:, 0:2, :], ALU.add)
                    last = v.tensor_tensor(
                        Vx[:, bass.ds(c * CT + i, 1), 0:NH * VW].rearrange("p t (h n) -> p (t h) n", n=VW)[:, :, 0:HD],
                        ps[:, FC + i % 3, 2 * D:3 * D].rearrange("p (h n) -> p h n", n=HD),
                        biasB[:, 2, :].rearrange("p (h n) -> p h n", n=HD), ALU.add)
                    last.then_inc(qk_ev, 1)
                if more:
                    norm_rows(1, 1, X1, c + 1)
                dve.wait_ge(qk_ev, c * CT + CT + 4)
                half = HD // 2
                for n in range(2):
                    x4 = qk[:, n, :, :].rearrange("p t (h d) -> p t h d", d=HD)
                    c4 = qc[:, n, :, :].rearrange("p t (h d) -> p t h d", d=HD)
                    s4 = qs[:, n, :, :].rearrange("p t (h d) -> p t h d", d=HD)
                    cos = rope[:, 0, bass.ds(c * CT, CT), :].unsqueeze(2)
                    sin = rope[:, 1, bass.ds(c * CT, CT), :].unsqueeze(2)
                    v.tensor_tensor(c4, x4, cos.broadcast_to([P, CT, NH, HD]), ALU.mult)
                    v.tensor_tensor(s4[:, :, :, 0:half], x4[:, :, :, half:HD],
                                    sin[:, :, :, 0:half].broadcast_to([P, CT, NH, half]), ALU.mult)
                    last = v.tensor_tensor(s4[:, :, :, half:HD], x4[:, :, :, 0:half],
                                           sin[:, :, :, half:HD].broadcast_to([P, CT, NH, half]), ALU.mult)
                steps = [0]

                def step(ins):
                    steps[0] += 1
                    ins.then_inc(q_step, 1)
                    dve.wait_ge(q_step, c * QSTEPS + steps[0])

                def flat(t):
                    return t.rearrange("p n t d -> p (n t d)")

                step(last)
                step(v.tensor_tensor(flat(qk[:, :, :, :]), flat(qc[:, :, :, :]), flat(qs[:, :, :, :]), ALU.add))
                dve.wait_ge(terms_k, c + 1)
                step(v.tensor_copy(flat(part[:, 0, :, :, :]), flat(qk[:, :, :, :])))
                step(v.tensor_tensor(flat(qc[:, :, :, :]), flat(qk[:, :, :, :]), flat(part[:, 0, :, :, :]), ALU.subtract))
                step(v.tensor_copy(flat(part[:, 1, :, :, :]), flat(qc[:, :, :, :])))
                assert steps[0] == QSTEPS
                v.tensor_tensor(flat(part[:, 2, :, :, :]), flat(qc[:, :, :, :]), flat(part[:, 1, :, :, :]),
                                ALU.subtract).then_inc(parts_ready, 1)
                dve.wait_ge(parts_ready, c + 1)
                dve.wait_ge(q_tr, c * 4 + 4)
                tq = terms[:, 0, :, :, :].rearrange("p t h r -> p (t h) r")
                for r in range(len(Q_PART)):
                    last = v.tensor_copy(tq[:, :, r * HD:(r + 1) * HD],
                                         part[:, Q_PART[r], 0, :, :].rearrange("p t (h d) -> p (t h) d", d=HD))
                last.then_inc(terms_q, 1)

            row_stats(X1, 0)
            norm_rows(1, 1, X1, 0)
            with dve.Fori(0, NC - 1) as c:
                project_chunk(c, True)
            project_chunk(NC - 1, False)

            def row_max(n, c):
                u = n % A_STEP
                h, q, half_ = u % 2, u // 4, u // 2 % 2
                dve.wait_ge(a_ready, c * A_IT + n + 1)
                at = (h * CT + q) * 2 + half_
                v.tensor_reduce(mh[:, n // A_STEP % 2, at:at + 1],
                                ps[:, A0 + 2 * (n % 2):A0 + 2 * (n % 2) + 2, :].rearrange("p a b -> p (a b)"),
                                AX.X, ALU.max).then_inc(a_free, 1)

            MSTEPS = 4

            def cut_max(i, c):
                b = i % 2
                done = [0]

                def step(ins):
                    done[0] += 1
                    ins.then_inc(m_step, 1)
                    dve.wait_ge(m_step, (c * PAIRS + i) * MSTEPS + done[0])

                parts = mp[:, b, :].rearrange("p (h r q) -> p h r q", h=2, r=3)
                m3 = nm[:, b, :].rearrange("p (h q) -> p h q", h=2)
                r3 = nr[:, b, :].rearrange("p (h q) -> p h q", h=2)
                dve.wait_ge(a_free, c * A_IT + (i + 1) * A_STEP)
                step(v.tensor_reduce(nm[:, b, :], mh[:, b, :].rearrange("p (m n) -> p m n", n=2), AX.X, ALU.max,
                                     negate=True))
                step(v.tensor_copy(parts[:, :, 0, :], m3))
                step(v.tensor_tensor(r3, m3, parts[:, :, 0, :], ALU.subtract))
                step(v.tensor_copy(parts[:, :, 1, :], r3))
                v.tensor_tensor(parts[:, :, 2, :], r3, parts[:, :, 1, :], ALU.subtract).then_inc(mp_ready, 1)
                assert done[0] == MSTEPS

            def take_rows(i, c):
                dve.wait_ge(rows_set, c * PAIRS + i + 1)
                v.tensor_copy(mrow[:, i % 2, :], psb[0:2 * 3 * CT, MISC, 0:P])\
                    .then_inc(rows_ready, 1)

            def normalise(i, c):
                dve.wait_ge(sel_done, c * PAIRS + i + C_TWO + 1)
                o = ps[:, MISC, 0:CT * 2 * VW].rearrange("p (q h n) -> p q h n", q=CT, h=2)
                v.reciprocal(rec[:, i % 2], o[:, :, :, HD:VW]).then_inc(rec_ready, 1)
                dve.wait_ge(rec_ready, c * PAIRS + i + 1)
                v.tensor_tensor(AO[:, bass.ds(c * CT, CT), i * 2 * HD:(i + 1) * 2 * HD]
                                .rearrange("p q (h d) -> p q h d", h=2),
                                o[:, :, :, 0:HD], rec[:, i % 2].broadcast_to([P, CT, 2, HD]), ALU.mult)\
                    .then_inc(misc_free, 1)

            def window(w, c, last):
                for pos in range(A_STEP):
                    n = w * A_STEP + LEAD + pos
                    if not last or n < A_IT:
                        row_max(n, c)
                    if pos == PREP_AT and (not last or w < PAIRS - 1):
                        cut_max(w + 1, c)
                    if pos == NORM_AT and w:
                        normalise(w - 1, c)
                    if pos == ROWS_AT and (not last or w < PAIRS - 1):
                        take_rows(w + 1, c)
                if w == PAIRS - 1:
                    normalise(w, c)

            for n in range(LEAD):
                row_max(n, 0)
                if n == A_STEP - 1:
                    cut_max(0, 0)
            take_rows(0, 0)
            with dve.Fori(0, NC - 1) as c:
                for w in range(PAIRS):
                    window(w, c, False)
            for w in range(PAIRS):
                window(w, NC - 1, True)

            dve.wait_ge(xb_ready, 2 * NC)
            with dve.Fori(0, NC) as c:
                dve.wait_ge(xt_done, c + NC * 2 + C_ONE)
                v.tensor_copy(xn[:, :, :], chunk(AO, c)).then_inc(xn_ready, 1)
                dve.wait_ge(pr_ready, c + NC + 1)
                v.tensor_tensor(chunk(X2, c), ps[:, PR, :].rearrange("p (t d) -> p t d", t=CT), chunk(X2, c),
                                ALU.add).then_inc(x1_ready, 1)
            dve.wait_ge(x1_ready, 2 * NC + C_ONE)
            ffn(1)

        @block.scalar
        def _(act):
            a = nc.scalar
            def take_xt(slot, c):
                act.wait_ge(xt_done, c + NC * slot + C_ONE + 1)
                a.copy(XT, ps[:, TP, :]).then_inc(xt_ready, 1)

            def gelu(p, c, i):
                n = (c + p * NC) * CT + i
                act.wait_ge(fc_ready, n + 1)
                act.wait_ge(n_ready, n + 1)
                a.activation(hid[:, i, :], ps[:, FC + i, :], ACT.Gelu).then_inc(h_ready, 1)

            def take_ht(p, c, i):
                act.wait_ge(nt_done, (c + p * NC) * CT + i + CT + 1)
                a.copy(hT[:, i, :, :], ps[:, TR + i % 2, :].rearrange("p (k n) -> p k n", k=KH)).then_inc(nt_ready, 1)

            def ffn(p):
                take_xt(3 * p, 0)
                for i in range(CT):
                    gelu(p, 0, i)
                with act.Fori(0, NC - 1) as c:
                    take_xt(3 * p, c + 1)
                    for i in range(CT):
                        take_ht(p, c, i)
                        gelu(p, c + 1, i)
                for i in range(CT):
                    take_ht(p, NC - 1, i)

            ffn(0)

            act.wait_ge(v_set, 2)

            def project_chunk(c, more):
                if more:
                    take_xt(1, c + 1)
                act.wait_ge(parts_ready, c + 1)
                act.wait_ge(k_tr, c * 4 + 4)
                tk = terms[:, 1, :, :, :].rearrange("p t h r -> p (t h) r")
                for r in range(len(K_PART)):
                    last = a.copy(tk[:, :, r * HD:(r + 1) * HD],
                                  part[:, K_PART[r], 1, :, :].rearrange("p t (h d) -> p (t h) d", d=HD))
                last.then_inc(terms_k, 1)
                for to, banks, done, out_of in ((QT, (PR, FC + 3), q_tr, qt_ev), (KT, (TR, TR + 1), k_tr, kt_ev)):
                    for e in range(4):
                        act.wait_ge(done, c * 4 + e + 5)
                        a.copy(to[:, 2 * e:2 * e + 2, bass.ds(c * CS, CS)],
                               psb[:, banks[e % 2], :].rearrange("p (j n) -> p j n", j=2)).then_inc(out_of, 1)

            take_xt(1, 0)
            with act.Fori(0, NC - 1) as c:
                project_chunk(c, True)
            project_chunk(NC - 1, False)

            def exp_unit(k, c):
                act.wait_ge(b_ready, c * B_IT + k + 1)
                if k % BATCH == 0:
                    act.wait_ge(pv_done, c * PV_IT + k // BATCH + 1)
                a.activation(ring[:, k % PRING, :], ps[:, B0 + k % 2, :], ACT.Exp, scale=SCALE).then_inc(p_ready, 1)

            def take_out(i, c):
                act.wait_ge(pv_done, c * PV_IT + (i + 1) * NB + PRING // BATCH)
                act.wait_ge(sel_done, c * PAIRS + i + 1)
                a.copy(outT[:, i % 2, :], ps[:, PO, :]).then_inc(po_free, 1)

            with act.Fori(0, NC) as c:
                for w in range(PAIRS):
                    for k in range(B_STEP):
                        exp_unit(w * B_STEP + k, c)
                        if k == 5 and w:
                            take_out(w - 1, c)
                take_out(PAIRS - 1, c)

            with act.Fori(0, NC) as c:
                take_xt(2, c)
            ffn(1)

        @block.tensor
        def _(pe):
            t = nc.tensor

            pe.wait_ge(consts, 1)
            pe.wait_ge(setup_v, 1)
            t.matmul(ps[:, TP, 0:2], ones[:, :], asum[:, :], start=True, stop=True).then_inc(setup_p, 1)
            pe.wait_ge(setup_v, 5)
            for n in range(2):
                for k in range(KH):
                    last = t.transpose(psb[:, TR + n, k * P:(k + 1) * P], tern[:, n, k * P:(k + 1) * P], identb[:, :])
            last.then_inc(setup_p, 1)
            pe.wait_ge(setup_v, 7)
            pe.wait_ge(w_in, 16 * W_DMAS)
            for n in range(4):
                t.transpose(ps[:, TR, n * P:(n + 1) * P], w_n[:, n, :], ident[:, :])
            for k in range(KH):
                last = t.matmul(ps[:, PR, 0:D], lnbB[:, k, :], WpT[:, k, :], start=(k == 0), stop=(k == KH - 1))
            last.then_inc(setup_p, 1)
            pe.wait_ge(setup_v, SETUP_V)

            def put_xt(slot, c):
                pe.wait_ge(xn_ready, c + NC * slot + 1)
                pe.wait_ge(xt_ready, c + NC * slot + C_ONE)
                for i in range(CT):
                    last = t.transpose(ps[:, TP, i * P:(i + 1) * P], xn[:, i, :], ident[:, :])
                last.then_inc(xt_done, 1)
                pe.wait_ge(xt_ready, c + NC * slot + C_ONE + 1)

            def expand(p, c, i):
                pe.wait_ge(h_ready, (c + p * NC) * CT + i + 1)
                t.matmul(ps[:, FC + i, :], XT[:, i * P:(i + 1) * P], WfcT[:, :], start=True, stop=True)\
                    .then_inc(fc_ready, 1)

            def turn(p, c, i):
                n = (c + p * NC) * CT + i
                pe.wait_ge(n_ready, n + CT + 1)
                pe.wait_ge(nt_ready, n + 1)
                for k in range(KH):
                    last = t.transpose(ps[:, TR + i % 2, k * P:(k + 1) * P], hn[:, i, k * P:(k + 1) * P],
                                       ident[:, :])
                last.then_inc(nt_done, 1)

            def contract(p, c, i):
                pe.wait_ge(nt_ready, (c + p * NC) * CT + i + C_TWO + 1)
                if i == 0:
                    pe.wait_ge(x1_ready, c + 2 * p * NC + C_ONE)
                for k in range(KH):
                    last = t.matmul(ps[:, PR, i * D:(i + 1) * D], hT[:, i, k, :], WpS[:, k, :],
                                    start=(k == 0), stop=(k == KH - 1))
                if i == CT - 1:
                    last.then_inc(pr_ready, 1)

            def ffn_chunk(p, c, more):
                if more:
                    put_xt(3 * p, c + 1)
                for i in range(CT):
                    turn(p, c, i)
                    if more:
                        expand(p, c + 1, i)
                    if i:
                        contract(p, c, i - 1)
                contract(p, c, CT - 1)

            def ffn(p):
                put_xt(3 * p, 0)
                for i in range(CT):
                    expand(p, 0, i)
                with pe.Fori(0, NC - 1) as c:
                    ffn_chunk(p, c, True)
                ffn_chunk(p, NC - 1, False)

            ffn(0)

            pe.wait_ge(h_ready, NT + C_TILE)
            pe.wait_ge(nt_ready, NT + C_TWO)
            pe.wait_ge(x1_ready, NC + C_ONE)

            def project_chunk(c, more):
                for i in range(CT):
                    pe.wait_ge(qk_ev, c * CT + (CT if i < 3 else 1 + CT))
                    t.matmul(ps[:, FC + i % 3, 0:3 * D], XT[:, i * P:(i + 1) * P],
                             WT[:, 0:3, :].rearrange("p n d -> p (n d)"), start=True, stop=True).then_inc(qkv_ready, 1)
                if more:
                    put_xt(1, c + 1)
                for n, banks, ready, free, done in ((0, (PR, FC + 3), terms_q, qt_ev, q_tr),
                                                    (1, (TR, TR + 1), terms_k, kt_ev, k_tr)):
                    pe.wait_ge(ready, c + C_ONE + 1)
                    for e in range(4):
                        pe.wait_ge(free, c * 4 + e + 1)
                        for j in range(2):
                            for i in range(CT):
                                last = t.transpose(psb[:, banks[e % 2], (j * CT + i) * P:(j * CT + i + 1) * P],
                                                   terms[:, n, i, 4 * e + 2 * j:4 * e + 2 * j + 2, :]
                                                   .rearrange("p h r -> p (h r)"), identb[:, :])
                        last.then_inc(done, 1)

            put_xt(1, 0)
            with pe.Fori(0, NC - 1) as c:
                project_chunk(c, True)
            project_chunk(NC - 1, False)

            pe.wait_ge(qk_ev, NT + C_TILE)
            for m in range(WARM):
                t.matmul(ps[:, FC + m % 3, :], identb[:, :], tern[:, 0, :], start=True, stop=True)
            pe.wait_ge(kt_ev, 4 * NC + C_TWO)
            pe.wait_ge(qt_ev, 4 * NC + C_TWO)
            pe.wait_ge(xt_ready, 2 * NC + C_ONE)

            def max_mm(m, c):
                n, x = m // 2, m % 2
                i, u = n // A_STEP, n % A_STEP
                j = i % PAIRS
                h, q, half = u % 2, u // 4, u // 2 % 2
                if x == 0:
                    if u == 0:
                        pe.wait_ge(q_in[j], (c + i // PAIRS + 1) * 32)
                    if type(c) is not int or n >= 2:
                        pe.wait_ge(a_free, c * A_IT + n - 1)
                mm = t.matmul(ps[:, A0 + 2 * (n % 2) + x, :], QS[:, h, j, q * P:(q + 1) * P],
                              KT[:, j, (2 * half + x) * 512:(2 * half + x + 1) * 512], start=True, stop=True)
                if x:
                    mm.then_inc(a_ready, 1)

            def exp_mm(i, k, c):
                b, r4 = k // BATCH, k % BATCH
                h, kt = r4 // 2, 2 * b + r4 % 2
                if k == 0:
                    pe.wait_ge(m_in[i], (c + 1) * 32)
                pe.wait_ge(p_ready, c * B_IT + i * B_STEP + k + 1)
                t.matmul(ps[:, B0 + k % 2, :], KT[:, i, kt * P:(kt + 1) * P], QS[:, h, i, :],
                         start=True, stop=True).then_inc(b_ready, 1)

            def pv_batch(i, b, c):
                if b == 0:
                    pe.wait_ge(po_free, c * PAIRS + i + C_ONE)
                pe.wait_ge(p_ready, c * B_IT + i * B_STEP + (b + 1) * BATCH + C_TWO)
                for r4 in range(BATCH):
                    h, kt = r4 // 2, 2 * b + r4 % 2
                    col = (2 * i + h) * VW
                    mm = t.matmul(ps[32 * r4:32 * r4 + 32, PO, :], Vx[:, kt, col:col + 32],
                                  ring[:, (b * BATCH + r4) % PRING, :], start=(b == 0), stop=(b == NB - 1))
                mm.then_inc(pv_done, 1)

            def select(i, c, rows):
                pe.wait_ge(po_free, c * PAIRS + i + C_ONE + 1)
                pe.wait_ge(rows_ready, c * PAIRS + rows)
                pe.wait_ge(misc_free, c * PAIRS + i + C_ONE)
                for q in range(CT):
                    mm = t.matmul(ps[:, MISC, q * 2 * VW:(q + 1) * 2 * VW], outT[:, i % 2, q * P:(q + 1) * P],
                                  pick[:, :], start=True, stop=True)
                mm.then_inc(sel_done, 1)

            def turn_max(i, c):
                pe.wait_ge(mp_ready, c * PAIRS + i + 1)
                n = 2 * 3 * CT
                return t.transpose(psb[0:n, MISC, 0:P], mp[:, i % 2, :], identb[:, :])

            for m in range(2 * LEAD):
                max_mm(m, 0)
            turn_max(0, 0).then_inc(rows_set, 1)

            def steps(c, last):
                for i in range(PAIRS):
                    for k in range(B_STEP):
                        exp_mm(i, k, c)
                        m = i * B_STEP + k + 2 * LEAD
                        if not last or m < 2 * A_IT:
                            max_mm(m, c)
                        if k % BATCH == BATCH - 1:
                            b = k // BATCH
                            if b:
                                pv_batch(i, b - 1, c)
                            elif i:
                                pv_batch(i - 1, NB - 1, c)
                            if b == SEL_BATCH and i:
                                select(i - 1, c, i + 1)
                            if b == MT_BATCH and (not last or i < PAIRS - 1):
                                pe.wait_ge(misc_free, c * PAIRS + i + C_ONE)
                                turn_max(i + 1, c).then_inc(rows_set, 1)
                pv_batch(PAIRS - 1, NB - 1, c)
                select(PAIRS - 1, c, PAIRS + (0 if last else 1))

            with pe.Fori(0, NC - 1) as c:
                steps(c, False)
            steps(NC - 1, True)

            pe.wait_ge(misc_free, NC * PAIRS + C_ONE)
            with pe.Fori(0, NC) as c:
                put_xt(2, c)
                pe.wait_ge(x1_ready, c + NC + C_ONE)
                for i in range(CT):
                    last = t.matmul(ps[:, PR, i * D:(i + 1) * D], XT[:, i * P:(i + 1) * P], WT[:, 3, :],
                                    start=True, stop=True)
                last.then_inc(pr_ready, 1)
            ffn(1)


_INS = ['L0_attn_x', 'L0_attn_wq', 'L0_attn_bq', 'L0_attn_wk', 'L0_attn_bk', 'L0_attn_wv', 'L0_attn_bv',
        'L0_attn_wo', 'L0_attn_bo', 'L0_ffn_W_fc', 'L0_ffn_ln_w', 'L0_ffn_ln_b', 'L0_ffn_W_proj']
_OUTS = [((1, S, D), 'float32')]


def kernel(**inputs):
    import numpy as _np
    import concourse.bacc as _bacc
    from concourse import mybir as _mybir
    from concourse.bass_utils import run_bass_kernel_spmd as _run

    nc = _bacc.Bacc("TRN2", target_bir_lowering=False, num_devices=1)
    arrays, args = {}, []
    for name in _INS:
        a = _np.ascontiguousarray(inputs[name])
        arrays[f"in_{name}_dram"] = a
        args.append(nc.dram_tensor(f"in_{name}_dram", a.shape, _mybir.dt.from_np(a.dtype), kind="ExternalInput").ap())
    for i, (shape, dtype) in enumerate(_OUTS):
        dt = _mybir.dt.from_np(_np.dtype(dtype))
        args.append(nc.dram_tensor(f"out_{i}_dram", shape, dt, kind="ExternalOutput").ap())
    macaron(nc, *args)
    r = _run(nc, [arrays], core_ids=[0])
    return r.results[0]["out_0_dram"]
```

```python
from contextlib import ExitStack

import numpy as np

import concourse.bass as bass
from concourse import mybir

F32 = mybir.dt.float32
BF16 = mybir.dt.bfloat16
ALU = mybir.AluOpType
ACT = mybir.ActivationFunctionType
AX = mybir.AxisListType

P = 128
S = 2048
D = 128
H = 512
NH = 16
HD = D // NH
NT = S // P
CT = 4
NC = NT // CT
CS = CT * P
KH = H // P
LN_EPS = 1e-5
ABS_EPS = 1e-6

Q_PART = (0, 1, 0, 1, 2, 0)
K_PART = (0, 1, 1, 0, 0, 2)
PART_ROWS = (0, 1)
LAST_ROW = (Q_PART.index(2), K_PART.index(2))
HR = 64
R_QK = len(Q_PART) * HD
R_ALL = R_QK + 3

PAIRS = NH // 2
SCALE = float(1.0 / np.sqrt(np.float32(HD)))
TURNS = 2 * PAIRS // 2
VW = HD + 1
VCOLS = NH * VW + 32 - VW

A_STEP = 2 * CT * 2
B_STEP = 2 * NT
BATCH = 4
NB = B_STEP // BATCH
LEAD = 23
PRING = 16

SHARED_AT = 12
SPLIT = 2 * SHARED_AT
TOP_AT = 2 * A_STEP - LEAD
OUT_AT = 4

A_IT = PAIRS * A_STEP
B_IT = PAIRS * B_STEP
PV_IT = PAIRS * NB
SLOT_IT = PAIRS * (A_STEP + 1)


def unit_slot(n):
    return n + max(0, (n - LEAD - SHARED_AT) // A_STEP + 2)


def shared_slot(w, last=False):
    units = LEAD + A_STEP * w + SHARED_AT
    return (min(units, A_IT) if last else units) + w + 1


TURN_ORDER = [("T", 0), ("T", 1), ("F", 0), ("T", 2), ("F", 1), ("F", 2), ("T", 3), ("F", 3)]
TURNED = {x: n for n, x in enumerate(TURN_ORDER)}
LATE = {(6, 5): ("T", 0), (6, 6): ("O", 0), (6, 7): ("T", 1), (7, 0): ("O", 1), (7, 1): ("F", 0),
        (7, 2): ("T", 2), (7, 3): ("O", 2), (7, 5): ("F", 1), (7, 7): ("F", 2)}

QSTEPS = 12
K_CUT = (9, 12)

WARM = 10
SETUP_V = 9
W_DMAS = 11

C_TILE = CT
C_TWO = 2
C_EXP = 3
C_ONE = 1
C_RING = PRING // BATCH


def rope_tables():
    inv = (1.0 / 10000.0 ** (np.arange(0, HD, 2, dtype=np.float32) / np.float32(HD))).astype(np.float32)
    ang = (np.arange(S, dtype=np.float32)[:, None] * inv[None, :]).astype(np.float32).astype(np.float64)
    cos = np.concatenate([np.cos(ang), np.cos(ang)], 1)
    sin = np.concatenate([-np.sin(ang), np.sin(ang)], 1)
    both = np.stack([cos, sin], 0).astype(np.float32)
    return np.ascontiguousarray(both.reshape(2, NT, P, HD).transpose(2, 0, 1, 3))


def macaron(nc, x, wq, bq, wk, bk, wv, bv, wo, bo, w_fc, ln_w, ln_b, w_proj, out):
    rope_dram = nc.inline_tensor(rope_tables(), name="rope_tables").ap()

    with ExitStack() as ctx:
        def sb(name, shape, dt=F32):
            return ctx.enter_context(nc.sbuf_tensor(name, shape, dt))

        def sem(name):
            return ctx.enter_context(nc.semaphore(name))

        ps = ctx.enter_context(nc.psum_tensor("ps", [P, 8, 512], F32))
        psb = ps[:, :, :].bitcast(BF16)
        FC, TP = 0, 7
        PR = (6, 4)
        TR = (4, 5, 6)
        A0, EXP, PO = 0, (4, 5, 7), 6

        X = sb("X", [P, NT, D])
        X1 = sb("X1", [P, NT, D])
        X2 = sb("X2", [P, NT, D])
        AO = X
        Y = X1
        XB = sb("XB", [P, NT, D])
        ring = sb("ring", [P, PRING, CS])
        hid = ring[:, 0:KH, :]
        sq = ring[:, KH:2 * KH, :]
        sqsum = ring[:, 2 * KH:3 * KH - 1, :]
        XT = ring[:, 3 * KH - 1, :]
        xn = sb("xn", [P, CT, D])
        st = sb("st", [P, NT, 6])
        mv = sb("mv", [P, NT, 2])
        ve = sb("ve", [P, NT])
        rs = sb("rs", [P, NT])
        mean2 = sb("mean2", [P, CT])
        msq4 = sb("msq4", [P, CT])
        var4 = sb("var4", [P, CT])
        rsh = sb("rsh", [P, CT])
        eps = sb("eps", [P, CT])
        half_neg = sb("half_neg", [P, CT])
        ident = sb("ident", [P, P])
        identb = sb("identb", [P, P], BF16)
        ones = sb("ones", [P, P])
        wfc_n = sb("wfc_n", [P, KH, D])
        wpj_n = sb("wpj_n", [P, H])
        tern = sb("tern", [P, 2, H], BF16)
        below = sb("below", [P, 2, H], BF16)
        asum = sb("asum", [P, 2])
        gam = sb("gam", [P, 2])
        thr = sb("thr", [P, 2])
        nthr = sb("nthr", [P, 2])
        WfcT = sb("WfcT", [P, H])
        WpT = sb("WpT", [P, KH, D])
        WpS = sb("WpS", [P, KH, D])
        wbar = sb("wbar", [P, D])
        WpC = sb("WpC", [P, KH, D + 1])
        lnw = sb("lnw", [P, KH])
        lnb = sb("lnb", [P, KH])
        lnbB = sb("lnbB", [P, KH, P])
        halfb = sb("halfb", [P, D])
        w_n = sb("w_n", [P, 4, D])
        WT = sb("WT", [P, 4, D])
        biasB = sb("biasB", [P, 4, D])
        rope = sb("rope", [P, 2, NT, HD])
        qk = ring[:, 4:6, :].rearrange("p n (t d) -> p n t d", t=CT)
        qc = X[:, 0:2 * CT, :].rearrange("p (n t) d -> p n t d", n=2)
        qs = X[:, 2 * CT:4 * CT, :].rearrange("p (n t) d -> p n t d", n=2)
        terms = sb("terms", [P, 2, CT, NH, HR], BF16)
        KT = sb("KT", [P, PAIRS, S], BF16)
        QT = sb("QT", [P, PAIRS, S], BF16)
        XF = QT[:, 0:2, :].rearrange("p j n -> p (j n)").bitcast(F32)
        XO = QT[:, 2, 0:2 * CS].bitcast(F32).rearrange("p (i d) -> p i d", d=D)
        XOT = QT[:, 3, 0:2 * CS].bitcast(F32)
        QS = sb("QS", [P, 2, PAIRS, CS], BF16)
        Vx = sb("Vx", [P, NT, VCOLS])
        mh = sb("mh", [P, 2, A_STEP])
        top = sb("top", [P, 2 * CT])
        cuts = sb("cuts", [P, 2, 2 * CT])
        zeros = sb("zeros", [P, 2 * CT])
        warm_in = sb("warm_in", [P, H], BF16)
        table = sb("table", [P, 2])
        mp = sb("mp", [P, 2, 2 * 3 * CT], BF16)
        mrow = sb("mrow", [2 * 3 * CT, 2, P], BF16)
        outT = sb("outT", [P, 2, CS])
        pick = sb("pick", [P, 2 * VW])
        rec = sb("rec", [P, 2, CT, 2, 1])

        x_in = sem("x_in")
        w_in = sem("w_in")
        wf_in = sem("wf_in")
        ident0 = sem("ident0")
        consts = sem("consts")
        setup_v = sem("setup_v")
        setup_p = sem("setup_p")
        ln_mv = sem("ln_mv")
        ln_ve = sem("ln_ve")
        ln_rs = sem("ln_rs")
        xn_ready = sem("xn_ready")
        xt_done = sem("xt_done")
        xt_ready = sem("xt_ready")
        fc_ready = sem("fc_ready")
        h_ready = sem("h_ready")
        sq_ready = sem("sq_ready")
        hid_used = sem("hid_used")
        h_var = sem("h_var")
        h_rs = sem("h_rs")
        pr_ready = sem("pr_ready")
        x1_ready = sem("x1_ready")
        xb_ready = sem("xb_ready")
        qkv_ready = sem("qkv_ready")
        qk_ev = sem("qk_ev")
        q_step = sem("q_step")
        sin_ready = sem("sin_ready")
        terms_k = sem("terms_k")
        terms_q = sem("terms_q")
        t_done = sem("t_done")
        t_ev = sem("t_ev")
        v_set = sem("v_set")
        q_in = [sem(f"q_in{j}") for j in range(PAIRS)]
        m_in = [sem(f"m_in{j}") for j in range(PAIRS)]
        a_ready = sem("a_ready")
        a_free = sem("a_free")
        b_ready = sem("b_ready")
        p_ready = sem("p_ready")
        pv_done = sem("pv_done")
        po_free = sem("po_free")
        m_step = sem("m_step")
        top_ready = sem("top_ready")
        mp_ready = sem("mp_ready")
        rows_ready = sem("rows_ready")
        rec_ready = sem("rec_ready")
        xo_ready = sem("xo_ready")
        turned = sem("turned")
        taken = sem("taken")
        o_ready = sem("o_ready")
        y_out = sem("y_out")

        block = ctx.enter_context(nc.Block())

        def late_banks(c):
            return (PR[1] + 1, PR[1]) if c == NC - 1 else (A0 + 1, A0 + 3)

        def chunk(t, c):
            return t[:, bass.ds(c * CT, CT), :]

        @block.sync
        def _(sp):
            sp.dma_start(wfc_n[:, :, :], w_fc.rearrange("(k p) d -> p k d", p=P)).then_inc(wf_in, 16)
            sp.dma_start(wpj_n[:, :], w_proj).then_inc(wf_in, 16)
            sp.dma_start(X[:, :, :], x.rearrange("a (t p) d -> p (a t) d", p=P)).then_inc(x_in, 16)

            def rows(i, c):
                j = i % PAIRS
                sp.wait_ge(rows_ready, c * PAIRS + i + 1)
                for h in range(2):
                    dst = QS[HR * h + R_QK:HR * h + R_ALL, h, j, :].rearrange("r (q n) -> r q n", q=CT)
                    sp.dma_start(dst, mrow[h * 3 * CT:(h + 1) * 3 * CT, i % 2, :]).then_inc(m_in[j], 16)

            rows(0, 0)
            with sp.Fori(0, NC - 1) as c:
                for i in range(1, PAIRS + 1):
                    rows(i, c)
            for i in range(1, PAIRS):
                rows(i, NC - 1)

            with sp.Fori(0, NC) as c:
                sp.wait_ge(x1_ready, c + 2 * NC + C_TWO + 1)
                sp.dma_start(out.rearrange("a (t p) d -> p (a t) d", p=P)[:, bass.ds(c * CT, CT), :],
                             chunk(Y, c)).then_inc(y_out, 16)
            sp.wait_ge(y_out, 16 * NC)

        @block.gpsimd
        def _(pool):
            g = nc.gpsimd
            for free, credit in ((xt_done, C_ONE), (xt_ready, C_ONE), (h_ready, C_TILE), (pr_ready, C_ONE),
                                 (sq_ready, C_ONE), (hid_used, C_ONE),
                                 (x1_ready, C_TWO), (qk_ev, C_TILE), (terms_k, C_ONE), (terms_q, C_ONE),
                                 (t_done, TURNS), (t_ev, C_EXP), (p_ready, C_EXP), (pv_done, C_RING),
                                 (po_free, C_ONE)):
                pool.sem_inc(free, credit)
            g.memset(ident[:, :], 0.0)
            g.memset(identb[:, :], 0.0)
            g.memset(pick[:, :], 0.0).then_inc(ident0, 1)
            pool.wait_ge(ident0, 1)
            g.affine_select(out=ident[:, :], in_=ident[:, :], compare_op=ALU.not_equal, fill=1.0, base=0,
                            pattern=[[-1, P]], channel_multiplier=1)
            g.affine_select(out=identb[:, :], in_=identb[:, :], compare_op=ALU.not_equal, fill=1.0, base=0,
                            pattern=[[-1, P]], channel_multiplier=1)
            for par in range(2):
                g.affine_select(out=pick[:, :].rearrange("p (h n) -> p h n", h=2),
                                in_=pick[:, :].rearrange("p (h n) -> p h n", h=2),
                                compare_op=ALU.not_equal, fill=1.0, base=-32 * par,
                                pattern=[[-64, 2], [-1, VW]], channel_multiplier=1).then_inc(ident0, 1)
                pool.wait_ge(ident0, par + 2)
            g.memset(half_neg[:, :], -0.5)
            g.memset(zeros[:, :], 0.0)
            g.memset(warm_in[:, :], 1.0)
            g.memset(eps[:, :], LN_EPS)
            g.memset(WpC[:, :, D:D + 1], 1.0)
            g.memset(ones[:, :], 1.0).then_inc(consts, 1)
            pool.wait_ge(consts, 1)

            def ln_scale(which, c, b):
                n = c + NC * which + 1
                pool.wait_ge(ln_mv, n)
                t = slice(b * CT, (b + 1) * CT)
                g.tensor_tensor(ve[:, t], mv[:, t, 1], eps[:, :], ALU.add).then_inc(ln_ve, 1)
                pool.wait_ge(ln_ve, n)
                g.tensor_tensor(rs[:, t], ve[:, t], half_neg[:, :], ALU.pow).then_inc(ln_rs, 1)

            def residual(p, c):
                g.tensor_tensor(chunk(XB, c), chunk((X, X2)[p], c),
                                halfb[:, :].unsqueeze(1).broadcast_to([P, CT, D]), ALU.add).then_inc(xb_ready, 1)

            def ffn_chunk(p, c):
                residual(p, c)
                pool.wait_ge(h_var, c + p * NC + 1)
                g.tensor_tensor(rsh[:, :], var4[:, :], half_neg[:, :], ALU.pow).then_inc(h_rs, 1)

            def ffn(p):
                with pool.Fori(0, NC - 1) as c:
                    ffn_chunk(p, c)
                if p == 0:
                    ln_scale(1, 0, 0)
                ffn_chunk(p, NC - 1)

            for c in range(NC):
                ln_scale(0, c, c)
            g.memset(Vx[:, :, :], 0.0).then_inc(v_set, 1)
            pool.wait_ge(v_set, 1)
            g.memset(Vx[:, :, 0:NH * VW].rearrange("p t (h n) -> p t h n", n=VW)[:, :, :, HD:VW], 1.0)
            g.memset(QS[:, :, :, :], 0.0)
            g.memset(terms[:, 0, :, :, R_QK:HR], 0.0)
            g.memset(terms[:, 1, :, :, R_QK:HR], 1.0).then_inc(v_set, 1)
            pool.wait_ge(setup_v, SETUP_V)
            ffn(0)

            pool.wait_ge(w_in, 16 * W_DMAS)
            def project_chunk(c, more):
                if more:
                    ln_scale(1, c + 1, 0)
                pool.wait_ge(qk_ev, c * CT + 2 * CT)
                for n in range(2):
                    x4 = qk[:, n, :, :].rearrange("p t (h d) -> p t h d", d=HD)
                    s4 = qs[:, n, :, :].rearrange("p t (h d) -> p t h d", d=HD)
                    sin = rope[:, 1, bass.ds(c * CT, CT), :].unsqueeze(2)
                    half = HD // 2
                    g.tensor_tensor(s4[:, :, :, 0:half], x4[:, :, :, half:HD],
                                    sin[:, :, :, 0:half].broadcast_to([P, CT, NH, half]), ALU.mult)
                    g.tensor_tensor(s4[:, :, :, half:HD], x4[:, :, :, 0:half],
                                    sin[:, :, :, half:HD].broadcast_to([P, CT, NH, half]), ALU.mult)\
                        .then_inc(sin_ready, 1)
                g.tensor_tensor(chunk(X2, c), chunk(X1, c),
                                biasB[:, 3, :].unsqueeze(1).broadcast_to([P, CT, D]), ALU.add).then_inc(xb_ready, 1)

            with pool.Fori(0, NC - 1) as c:
                project_chunk(c, True)
            project_chunk(NC - 1, False)

            MSTEPS = 4

            def cut_max(i, c):
                done = [0]

                def step(ins):
                    done[0] += 1
                    ins.then_inc(m_step, 1)
                    pool.wait_ge(m_step, (c * PAIRS + i) * MSTEPS + done[0])

                def by_head(t):
                    return t.rearrange("p (h q) -> p h q", h=2)

                parts = mp[:, i % 2, :].rearrange("p (h r q) -> p h r q", h=2, r=3)
                whole, zero = by_head(top[:, :]), by_head(zeros[:, :])
                left, rest = by_head(cuts[:, 0, :]), by_head(cuts[:, 1, :])
                pool.wait_ge(top_ready, c * PAIRS + i + 1)
                step(g.tensor_tensor(parts[:, :, 0, :], zero, whole, ALU.subtract))
                step(g.tensor_tensor(left, whole, parts[:, :, 0, :], ALU.add))
                step(g.tensor_tensor(parts[:, :, 1, :], zero, left, ALU.subtract))
                step(g.tensor_tensor(rest, left, parts[:, :, 1, :], ALU.add))
                g.tensor_tensor(parts[:, :, 2, :], zero, rest, ALU.subtract).then_inc(mp_ready, 1)
                assert done[0] == MSTEPS

            def load_q(j, c):
                for h in range(2):
                    g.dma_start(QS[HR * h:HR * h + R_ALL, h, j, :],
                                QT[HR * h:HR * h + R_ALL, j, bass.ds(c * CS, CS)]).then_inc(q_in[j], 16)

            pool.wait_ge(t_ev, C_EXP + TURNS)
            for j in range(PAIRS):
                load_q(j, 0)
            cut_max(0, 0)
            cut_max(1, 0)
            with pool.Fori(1, NC) as c:
                for j in range(PAIRS):
                    pool.wait_ge(b_ready, c * B_IT - B_IT + (j + 1) * B_STEP)
                    load_q(j, c)
                    cut_max(j + 2 - PAIRS, c)
            for i in range(2, PAIRS):
                cut_max(i, NC - 1)

            for c in range(NC):
                ln_scale(2, c, c)
            ffn(1)

        @block.vector
        def _(dve):
            v = nc.vector
            def rows_of(src, c, i):
                return src[:, bass.ds(c * CT + i, 1), :].rearrange("p t d -> p (t d)")

            def row_stats(src, c, b):
                for i in range(CT):
                    v.bn_stats(st[:, b * CT + i, :], rows_of(src, c, i))
                dve.drain()
                for i in range(CT):
                    last = v.bn_aggr(mv[:, b * CT + i, :], st[:, b * CT + i, :])
                last.then_inc(ln_mv, 1)

            def norm_rows(which, src, c, b):
                dve.wait_ge(ln_rs, c + NC * which + 1)
                if which < 2:
                    dve.wait_ge(xt_done, c + NC * which + C_ONE)
                elif c:
                    dve.wait_ge(turned, TURNED["F", c - 1] + 1)
                for i in range(CT):
                    last = v.tensor_scalar(xn[:, i, :], rows_of(src, c, i), mv[:, b * CT + i, 0:1],
                                           rs[:, b * CT + i:b * CT + i + 1], ALU.subtract, ALU.mult)
                last.then_inc(xn_ready, 1)

            chain = [0]

            def link(ins):
                chain[0] += 1
                ins.then_inc(setup_v, 1)
                dve.wait_ge(setup_v, chain[0])

            dve.wait_ge(wf_in, 32)
            natural = (wfc_n[:, :, :].rearrange("p k d -> p (k d)"), wpj_n[:, :])
            v.tensor_reduce(asum[:, 0:1], natural[0], AX.X, ALU.add, apply_absolute_value=True)
            link(v.tensor_reduce(asum[:, 1:2], natural[1], AX.X, ALU.add, apply_absolute_value=True))
            dve.wait_ge(setup_p, 1)
            link(v.tensor_scalar(gam[:, :], ps[:, TP, 0:2], 1.0 / (H * D), ABS_EPS, ALU.mult, ALU.add))
            v.tensor_scalar(thr[:, :], gam[:, :], 0.5, None, ALU.mult)
            link(v.tensor_scalar(nthr[:, :], gam[:, :], -0.5, None, ALU.mult))
            for n in range(2):
                last = v.tensor_scalar(below[:, n, :], natural[n], nthr[:, n:n + 1], None, ALU.is_lt)
            link(last)
            for n in range(2):
                last = v.scalar_tensor_tensor(tern[:, n, :], natural[n], thr[:, n:n + 1], below[:, n, :],
                                              ALU.is_gt, ALU.subtract)
            link(last)
            dve.wait_ge(x_in, 16)
            row_stats(X, 0, 0)
            dve.wait_ge(setup_p, 2)
            v.tensor_copy(WfcT[:, :], psb[:, TR[0], 0:H])
            link(v.tensor_copy(WpT[:, :, :], psb[:, TR[1], 0:H].rearrange("p (k d) -> p k d", k=KH)))
            row_stats(X, 1, 1)
            norm_rows(0, X, 0, 0)
            dve.wait_ge(w_in, 16 * W_DMAS)
            dve.wait_ge(consts, 1)
            for k in range(KH):
                v.tensor_scalar(WpS[:, k, :], WpT[:, k, :], lnw[:, k:k + 1], None, ALU.mult)
                last = v.tensor_scalar(lnbB[:, k, :], ones[:, :], lnb[:, k:k + 1], None, ALU.mult)
            link(last)
            norm_rows(0, X, 1, 1)
            row_stats(X, 2, 2)
            row_stats(X, 3, 3)
            norm_rows(0, X, 2, 2)
            dve.wait_ge(setup_p, 3)
            v.tensor_copy(WT[:, :, :], ps[:, TR[0], :].rearrange("p (n d) -> p n d", n=4))
            v.tensor_scalar(halfb[:, :], ps[:, TR[1], 0:D], 0.5, None, ALU.mult)
            link(v.tensor_scalar(wbar[:, :], ps[:, TR[1], D:2 * D], 1.0 / H, None, ALU.mult))
            link(v.tensor_tensor(WpC[:, :, 0:D], WpS[:, :, :], wbar[:, :].unsqueeze(1).broadcast_to([P, KH, D]),
                                 ALU.subtract))
            assert chain[0] == SETUP_V, chain[0]
            norm_rows(0, X, 3, 3)
            def square(p, c, k):
                dve.wait_ge(h_ready, (c + p * NC) * KH + k + C_TILE + 1)
                v.tensor_tensor(sq[:, k, :], hid[:, k, :], hid[:, k, :], ALU.mult)

            def add_square(k):
                dve.drain()
                return v.tensor_tensor(sqsum[:, k - 1, :], sqsum[:, k - 2, :] if k > 1 else sq[:, 0, :],
                                       sq[:, k, :], ALU.add)

            def results(c):
                return ps[:, PR[c]:PR[c] + 2, 0:2 * (D + 2)].rearrange("p b (t n) -> p b t n", t=2)

            def by_bank(t):
                return t.rearrange("p (b t) -> p b t", b=2)

            def variance(p, c, parity):
                o = results(parity)
                dve.wait_ge(pr_ready, c + p * NC + C_ONE + 1)
                v.tensor_scalar(by_bank(mean2[:, :]), o[:, :, :, D], 2.0 / H, None, ALU.mult)
                v.tensor_scalar(by_bank(var4[:, :]), o[:, :, :, D + 1], 4.0 / H, 4.0 * LN_EPS, ALU.mult, ALU.add)
                dve.drain()
                v.tensor_tensor(msq4[:, :], mean2[:, :], mean2[:, :], ALU.mult)
                dve.drain()
                v.tensor_tensor(var4[:, :], var4[:, :], msq4[:, :], ALU.subtract)
                dve.drain()
                v.tensor_scalar(var4[:, :], var4[:, :], 4.0 * LN_EPS, None, ALU.max).then_inc(h_var, 1)

            def update(p, c, parity):
                o = results(parity)
                dst = (X1, Y)[p]
                dve.wait_ge(xb_ready, c + 2 * p * NC + 1)
                dve.wait_ge(h_rs, c + p * NC + 1)
                for i in range(CT):
                    last = v.scalar_tensor_tensor(rows_of(dst, c, i), o[:, i // 2, i % 2, 0:D],
                                                  rsh[:, i:i + 1], rows_of(XB, c, i), ALU.mult, ALU.add)
                last.then_inc(x1_ready, 1)

            def ffn(p):
                def chunk_and_next(c, parity):
                    square(p, c + 1, 0)
                    variance(p, c, parity)
                    square(p, c + 1, 1)
                    add_square(1)
                    square(p, c + 1, 2)
                    add_square(2)
                    update(p, c, parity)
                    square(p, c + 1, 3)
                    add_square(3).then_inc(sq_ready, 1)

                with dve.Fori(0, NC // 2 - 1) as d:
                    chunk_and_next(2 * d, 0)
                    chunk_and_next(2 * d + 1, 1)
                if p == 0:
                    dve.wait_ge(x1_ready, C_TWO + 1)
                    row_stats(X1, 0, 0)
                chunk_and_next(NC - 2, 0)
                if p == 0:
                    norm_rows(1, X1, 0, 0)
                variance(p, NC - 1, 1)
                update(p, NC - 1, 1)

            for k in range(KH):
                square(0, 0, k)
                if k:
                    last = add_square(k)
            last.then_inc(sq_ready, 1)
            ffn(0)

            dve.wait_ge(v_set, 2)
            dve.wait_ge(x1_ready, NC + C_TWO)

            def by_head(t, n):
                return t[:, n, :, :].rearrange("p t (h d) -> p (t h) d", d=HD)

            def term(n, r):
                return terms[:, n, :, :, :].rearrange("p t h r -> p (t h) r")[:, :, r * HD:(r + 1) * HD]

            def project_chunk(c, more):
                if more:
                    row_stats(X1, c + 1, 0)
                for i in range(CT):
                    dve.wait_ge(qkv_ready, c * CT + i + 1)
                    v.tensor_tensor(qk[:, :, i, :], ps[:, FC + i, 0:2 * D].rearrange("p (n d) -> p n d", n=2),
                                    biasB[:, 0:2, :], ALU.add)
                    last = v.tensor_tensor(
                        Vx[:, bass.ds(c * CT + i, 1), 0:NH * VW].rearrange("p t (h n) -> p (t h) n", n=VW)[:, :, 0:HD],
                        ps[:, FC + i, 2 * D:3 * D].rearrange("p (h n) -> p h n", n=HD),
                        biasB[:, 2, :].rearrange("p (h n) -> p h n", n=HD), ALU.add)
                    last.then_inc(qk_ev, 1)
                if more:
                    norm_rows(1, X1, c + 1, 0)
                done = [0]

                def step(ins):
                    done[0] += 1
                    ins.then_inc(q_step, 1)
                    return done[0]

                def after(n):
                    dve.wait_ge(q_step, c * QSTEPS + n)

                def cosine(n):
                    return step(v.tensor_tensor(qc[:, n, :, :].rearrange("p t (h d) -> p t h d", d=HD),
                                                qk[:, n, :, :].rearrange("p t (h d) -> p t h d", d=HD),
                                                rope[:, 0, bass.ds(c * CT, CT), :].unsqueeze(2)
                                                .broadcast_to([P, CT, NH, HD]), ALU.mult))

                def rotated(n, cos):
                    after(cos)
                    dve.wait_ge(sin_ready, 2 * c + n + 1)
                    return step(v.tensor_tensor(by_head(qk, n), by_head(qc, n), by_head(qs, n), ALU.add))

                def cut(n, r, whole, ready):
                    after(ready)
                    return step(v.tensor_copy(term(n, r), by_head(whole, n)))

                def rest(n, r, whole, ready):
                    after(ready)
                    return step(v.tensor_tensor(by_head(qc, n), by_head(whole, n), term(n, r), ALU.subtract))

                def last_part(n, r, ready):
                    after(ready)
                    return step(v.tensor_tensor(term(n, r), by_head(qc, n), term(n, 1), ALU.subtract))

                dve.wait_ge(qk_ev, c * CT + 2 * CT)
                cos_q = cosine(0)
                cos_k = cosine(1)
                q = rotated(0, cos_q)
                dve.wait_ge(t_done, c * TURNS + PAIRS // 2)
                q0 = cut(0, 0, qk, q)
                k = rotated(1, cos_k)
                left = rest(0, 0, qk, q0)
                v.tensor_copy(term(0, 2), term(0, 0))
                q1 = cut(0, 1, qc, left)
                v.tensor_copy(term(0, 5), term(0, 0))
                last_part(0, LAST_ROW[0], q1)
                v.tensor_copy(term(0, 3), term(0, 1)).then_inc(terms_q, 1)
                dve.wait_ge(t_done, c * TURNS + TURNS)
                k0 = cut(1, 0, qk, k)
                left = rest(1, 0, qk, k0)
                k1 = cut(1, 1, qc, left)
                k2 = last_part(1, LAST_ROW[1], k1)
                assert (k0, k2, done[0]) == (*K_CUT, QSTEPS)

            with dve.Fori(0, NC - 1) as c:
                project_chunk(c, True)
            project_chunk(NC - 1, False)

            def slot_banks(s):
                return slice(A0 + 2 * (s % 2), A0 + 2 * (s % 2) + 2)

            def row_max(n, c):
                s, u = unit_slot(n), n % A_STEP
                h, q, half_ = u % 2, u // 2 % CT, u // (2 * CT)
                dve.wait_ge(a_ready, c * SLOT_IT + s + 1)
                at = (h * CT + q) * 2 + half_
                v.tensor_reduce(mh[:, n // A_STEP % 2, at:at + 1],
                                ps[:, slot_banks(s), :].rearrange("p a b -> p (a b)"),
                                AX.X, ALU.max).then_inc(a_free, 1)

            def whole_max(i, c):
                dve.wait_ge(a_free, c * SLOT_IT + unit_slot((i + 1) * A_STEP - 1) + 1)
                if type(c) is not int or i:
                    dve.wait_ge(mp_ready, c * PAIRS + i)
                v.tensor_reduce(top[:, :], mh[:, i % 2, :].rearrange("p (m n) -> p m n", n=2), AX.X, ALU.max)\
                    .then_inc(top_ready, 1)

            def shared(w, c, last=False):
                s = shared_slot(w, last)
                dve.wait_ge(a_ready, c * SLOT_IT + s + 1)
                if not last or w < PAIRS - 1:
                    done = v.tensor_copy(mrow[:, (w + 1) % 2, :], psb[0:2 * 3 * CT, A0 + 2 * (s % 2) + 1, 0:P])
                    done.then_inc(rows_ready, 1)
                if type(c) is int and w <= 0 and not last:
                    dve.wait_ge(rows_ready, w + 2)
                    dve.sem_inc(a_free, 1)
                    return
                i = w - 1
                o = ps[:, A0 + 2 * (s % 2), 0:CT * 2 * VW].rearrange("p (q h n) -> p q h n", q=CT, h=2)
                v.reciprocal(rec[:, i % 2], o[:, :, :, HD:VW]).then_inc(rec_ready, 1)
                dve.wait_ge(rec_ready, c * PAIRS + i + 1)
                v.tensor_tensor(AO[:, bass.ds(c * CT, CT), i * 2 * HD:(i + 1) * 2 * HD]
                                .rearrange("p q (h d) -> p q h d", h=2),
                                o[:, :, :, 0:HD], rec[:, i % 2].broadcast_to([P, CT, 2, HD]), ALU.mult)\
                    .then_inc(a_free, 1)

            def steps(w, start, stop, c, last=False):
                for pos in range(start, stop):
                    n = w * A_STEP + LEAD + pos
                    if not last or n < A_IT:
                        row_max(n, c)
                    if pos == TOP_AT and (not last or w < PAIRS - 1):
                        whole_max(w + 1, c)
                    if pos == SHARED_AT - 1:
                        shared(w, c, last)

            for n in range(LEAD):
                row_max(n, 0)
                if n == A_STEP:
                    whole_max(0, 0)
                if n == LEAD - A_STEP + SHARED_AT - 1:
                    shared(-1, 0)
            steps(0, 0, SHARED_AT, 0)
            with dve.Fori(0, NC - 1) as c:
                steps(0, SHARED_AT, A_STEP, c)
                for w in range(1, PAIRS):
                    steps(w, 0, A_STEP, c)
                steps(PAIRS, 0, SHARED_AT, c)
            steps(0, SHARED_AT, A_STEP, NC - 1, True)
            for w in range(1, PAIRS - 1):
                steps(w, 0, A_STEP, NC - 1, True)

            def output_rows(c):
                if c:
                    dve.wait_ge(turned, TURNED["T", c - 1] + 1)
                v.tensor_copy(XO, chunk(AO, c)).then_inc(xo_ready, 1)

            def take(kind, c):
                dve.wait_ge(turned, TURNED[kind, c] + 1)
                v.tensor_copy(XOT if kind == "T" else XF[:, c * CS:(c + 1) * CS], ps[:, late_banks(c)[0], :])\
                    .then_inc(taken, 1)

            def output_chunk(c):
                dve.wait_ge(o_ready, c + 1)
                v.tensor_tensor(chunk(X2, c), ps[:, late_banks(c)[1], :].rearrange("p (t d) -> p t d", t=CT),
                                chunk(X2, c), ALU.add).then_inc(x1_ready, 1)
                dve.wait_ge(x1_ready, c + NC + C_TWO + 1)
                row_stats(X2, c, c)

            for j in range(4):
                dve.wait_ge(q_in[j], NC * 32)
            dve.wait_ge(a_free, (NC - 1) * SLOT_IT + shared_slot(0) + 1)
            dve.wait_ge(xb_ready, 2 * NC)
            output_rows(0)
            take("T", 0)
            output_rows(1)
            output_chunk(0)
            take("T", 1)
            output_rows(2)
            norm_rows(2, X2, 0, 0)
            output_chunk(1)
            take("F", 0)
            norm_rows(2, X2, 1, 1)
            take("T", 2)
            output_chunk(2)
            shared(PAIRS - 1, NC - 1, True)
            take("F", 1)
            norm_rows(2, X2, 2, 2)
            take("F", 2)
            shared(PAIRS, NC - 1, True)
            dve.wait_ge(a_free, (NC - 1) * SLOT_IT + shared_slot(PAIRS, True) + 1)
            output_rows(3)
            take("T", 3)
            square(1, 0, 0)
            square(1, 0, 1)
            output_chunk(3)
            add_square(1)
            square(1, 0, 2)
            norm_rows(2, X2, 3, 3)
            add_square(2)
            square(1, 0, 3)
            add_square(3).then_inc(sq_ready, 1)
            take("F", 3)
            ffn(1)

        @block.scalar
        def _(act):
            a = nc.scalar
            act.dma_start(lnw[:, :], ln_w.rearrange("(k p) -> p k", p=P), allow_slow_non_contiguous=True)\
                .then_inc(w_in, 16)
            act.dma_start(lnb[:, :], ln_b.rearrange("(k p) -> p k", p=P), allow_slow_non_contiguous=True)\
                .then_inc(w_in, 16)
            for n, w in enumerate((wq, wk, wv, wo)):
                act.dma_start(w_n[:, n, :], w).then_inc(w_in, 16)
            for n, b in enumerate((bq, bk, bv, bo)):
                act.dma_start(biasB[:, n, :], b.partition_broadcast(P)).then_inc(w_in, 16)
            act.dma_start(rope[:, :, :, :], rope_dram).then_inc(w_in, 16)

            def take_xt(slot, c, to):
                act.wait_ge(xt_done, c + NC * slot + C_ONE + 1)
                a.copy(to, ps[:, TP, :]).then_inc(xt_ready, 1)

            def gelu(p, c, k):
                act.wait_ge(fc_ready, (c + p * NC) * KH + k + 1)
                a.activation(hid[:, k, :], ps[:, FC + k, :], ACT.Gelu).then_inc(h_ready, 1)

            def take_xf(c):
                take_xt(0, c, XF[:, c * CS:(c + 1) * CS])

            def ffn(p):
                if p == 0:
                    take_xf(0)
                for k in range(KH):
                    gelu(p, 0, k)
                if p == 0:
                    for c in range(1, NC):
                        take_xf(c)
                with act.Fori(1, NC) as c:
                    act.wait_ge(hid_used, c + p * NC + C_ONE)
                    act.wait_ge(sq_ready, c + p * NC + C_ONE)
                    for k in range(KH):
                        gelu(p, c, k)

            act.wait_ge(consts, 1)
            a.activation(table[:, 0:1], half_neg[:, 0:1], ACT.Gelu)
            ffn(0)

            act.wait_ge(v_set, 2)

            def project_chunk(c, more):
                if more:
                    take_xt(1, c + 1, XT)
                tk = terms[:, 1, :, :, :].rearrange("p t h r -> p (t h) r")

                def copy_part(to, r):
                    return a.copy(tk[:, :, to * HD:(to + 1) * HD], tk[:, :, r * HD:(r + 1) * HD])

                act.wait_ge(q_step, c * QSTEPS + K_CUT[0])
                for row in range(2, len(K_PART)):
                    if K_PART[row] == 0:
                        copy_part(row, PART_ROWS[0])
                act.wait_ge(q_step, c * QSTEPS + K_CUT[1])
                copy_part(K_PART.index(1, 2), PART_ROWS[1]).then_inc(terms_k, 1)
                for m in range(TURNS):
                    to, e = (QT, KT)[m // 4], m % 4
                    act.wait_ge(t_done, c * TURNS + m + TURNS + 1)
                    a.copy(to[:, 2 * e:2 * e + 2, bass.ds(c * CS, CS)],
                           psb[:, TR[m % 3], :].rearrange("p (j n) -> p j n", j=2)).then_inc(t_ev, 1)

            take_xt(1, 0, XT)
            with act.Fori(0, NC - 1) as c:
                project_chunk(c, True)
            project_chunk(NC - 1, False)

            def exp_unit(k, c):
                act.wait_ge(b_ready, c * B_IT + k + 1)
                if k % BATCH == 0:
                    act.wait_ge(pv_done, c * PV_IT + k // BATCH + 1)
                a.activation(ring[:, k % PRING, :], ps[:, EXP[k % C_EXP], :], ACT.Exp, scale=SCALE)\
                    .then_inc(p_ready, 1)

            def take_out(i, c):
                act.wait_ge(pv_done, c * PV_IT + (i + 1) * NB + C_RING)
                act.wait_ge(a_ready, c * SLOT_IT + shared_slot(i - 1, type(c) is int) + 1)
                a.copy(outT[:, i % 2, :], ps[:, PO, :]).then_inc(po_free, 1)

            def exps(w, start, stop, c):
                for k in range(start, stop):
                    exp_unit(w * B_STEP + k, c)
                    if k == OUT_AT and (w or type(c) is not int):
                        take_out(w - 1, c)

            exps(0, 0, SPLIT, 0)
            with act.Fori(0, NC - 1) as c:
                exps(0, SPLIT, B_STEP, c)
                for w in range(1, PAIRS):
                    exps(w, 0, B_STEP, c)
                exps(PAIRS, 0, SPLIT, c)
            exps(0, SPLIT, B_STEP, NC - 1)
            for w in range(1, PAIRS):
                exps(w, 0, B_STEP, NC - 1)
            take_out(PAIRS - 1, NC - 1)

            ffn(1)

        @block.tensor
        def _(pe):
            t = nc.tensor

            def put_xt(slot, c):
                pe.wait_ge(xn_ready, c + NC * slot + 1)
                pe.wait_ge(xt_ready, c + NC * slot + C_ONE)
                for i in range(CT):
                    last = t.transpose(ps[:, TP, i * P:(i + 1) * P], xn[:, i, :], ident[:, :])
                last.then_inc(xt_done, 1)

            def expand_block(p, c, k):
                pe.wait_ge(h_ready, (c + p * NC) * KH + k + 1)
                t.matmul(ps[:, FC + k, :], WfcT[:, k * P:(k + 1) * P], XF[:, bass.ds(c * CS, CS)],
                         start=True, stop=True).then_inc(fc_ready, 1)

            def expand(p, c):
                for k in range(KH):
                    expand_block(p, c, k)

            def warm(n, bank):
                for _ in range(n):
                    t.matmul(ps[:, bank, 0:H], identb[:, :], warm_in[:, :], start=True, stop=True)

            pe.wait_ge(consts, 1)
            pe.wait_ge(setup_v, 1)
            t.matmul(ps[:, TP, 0:2], ones[:, :], asum[:, :], start=True, stop=True).then_inc(setup_p, 1)
            pe.wait_ge(setup_v, 5)
            for n in range(2):
                for k in range(KH):
                    last = t.transpose(psb[:, TR[n], k * P:(k + 1) * P], tern[:, n, k * P:(k + 1) * P], identb[:, :])
            last.then_inc(setup_p, 1)
            warm(WARM, TR[2])

            def other_weights():
                pe.wait_ge(setup_v, 7)
                pe.wait_ge(w_in, 16 * W_DMAS)
                for n in range(4):
                    t.transpose(ps[:, TR[0], n * P:(n + 1) * P], w_n[:, n, :], ident[:, :])
                for k in range(KH):
                    t.matmul(ps[:, TR[1], 0:D], lnbB[:, k, :], WpT[:, k, :], start=(k == 0), stop=(k == KH - 1))
                for k in range(KH):
                    last = t.matmul(ps[:, TR[1], D:2 * D], ones[:, :], WpS[:, k, :], start=(k == 0),
                                    stop=(k == KH - 1))
                last.then_inc(setup_p, 1)

            put_xt(0, 0)
            pe.wait_ge(xt_ready, C_ONE + 1)
            expand(0, 0)
            put_xt(0, 1)
            other_weights()
            put_xt(0, 2)
            pe.wait_ge(xt_ready, C_ONE + 2)
            expand(0, 1)
            put_xt(0, 3)
            pe.wait_ge(xt_ready, NC + C_ONE)
            pe.wait_ge(setup_v, SETUP_V)

            def out_tile(i, parity):
                bank = PR[parity] + i // 2
                return ps[:, bank, i % 2 * (D + 2):(i % 2 + 1) * (D + 2)]

            def contract(p, c, parity):
                pe.wait_ge(h_ready, (c + p * NC + 1) * KH + C_TILE)
                pe.wait_ge(x1_ready, c + 2 * p * NC + C_TWO - 1)
                for i in range(CT):
                    for k in range(KH):
                        last = t.matmul(out_tile(i, parity)[:, 0:D + 1], hid[:, k, i * P:(i + 1) * P], WpC[:, k, :],
                                        start=(k == 0), stop=(k == KH - 1))
                last.then_inc(hid_used, 1)

            def sum_squares(p, c, parity):
                pe.wait_ge(sq_ready, c + p * NC + C_ONE + 1)
                for i in range(CT):
                    last = t.matmul(out_tile(i, parity)[:, D + 1:D + 2], sqsum[:, KH - 2, i * P:(i + 1) * P],
                                    ones[:, 0:1], start=True, stop=True)
                last.then_inc(pr_ready, 1)

            def ffn(p):
                def both(c, parity):
                    contract(p, c, parity)
                    sum_squares(p, c, parity)

                with pe.Fori(0, NC // 2 - 1) as d:
                    both(2 * d, 0)
                    if p:
                        pe.wait_ge(taken, TURNED["F", NC - 1] + 1)
                    expand(p, 2 * d + 2)
                    both(2 * d + 1, 1)
                    expand(p, 2 * d + 3)
                both(NC - 2, 0)
                both(NC - 1, 1)

            ffn(0)

            pe.wait_ge(h_ready, NC * KH + C_TILE)

            def project(c):
                pe.wait_ge(xt_ready, c + NC + C_ONE + 1)
                for i in range(CT):
                    pe.wait_ge(qk_ev, c * CT + i + 1)
                    t.matmul(ps[:, FC + i, 0:3 * D], XT[:, i * P:(i + 1) * P],
                             WT[:, 0:3, :].rearrange("p n d -> p (n d)"), start=True, stop=True).then_inc(qkv_ready, 1)

            def turn_terms(c, m):
                n, e = m // 4, m % 4
                if e == 0:
                    pe.wait_ge((terms_q, terms_k)[n], c + C_ONE + 1)
                pe.wait_ge(t_ev, c * TURNS + (C_EXP if m < 3 else m + 1))
                for j in range(2):
                    for i in range(CT):
                        last = t.transpose(psb[:, TR[m % 3], (j * CT + i) * P:(j * CT + i + 1) * P],
                                           terms[:, n, i, 4 * e + 2 * j:4 * e + 2 * j + 2, :]
                                           .rearrange("p h r -> p (h r)"), identb[:, :])
                last.then_inc(t_done, 1)

            put_xt(1, 0)
            project(0)
            pe.wait_ge(x1_ready, NC + C_TWO)
            with pe.Fori(0, NC - 1) as c:
                put_xt(1, c + 1)
                project(c + 1)
                for m in range(TURNS):
                    turn_terms(c, m)

            def slot_free(s, c):
                if type(c) is not int or c or s >= 2:
                    pe.wait_ge(a_free, c * SLOT_IT + s - 1)

            def max_mm(m, c):
                n, x = m // 2, m % 2
                i, u, s = n // A_STEP, n % A_STEP, unit_slot(n)
                j = i % PAIRS
                h, q, half = u % 2, u // 2 % CT, u // (2 * CT)
                if x == 0:
                    if u == 0:
                        pe.wait_ge(q_in[j], (c + i // PAIRS + 1) * 32)
                    slot_free(s, c)
                mm = t.matmul(ps[:, A0 + 2 * (s % 2) + x, :], QS[:, h, j, q * P:(q + 1) * P],
                              KT[:, j, (2 * half + x) * 512:(2 * half + x + 1) * 512], start=True, stop=True)
                if x:
                    mm.then_inc(a_ready, 1)

            def exp_mm(i, k, c):
                b, r4 = k // BATCH, k % BATCH
                h, kt = r4 // 2, 2 * b + r4 % 2
                n, j = i * B_STEP + k, i % PAIRS
                if k == 0:
                    pe.wait_ge(m_in[j], (c + i // PAIRS + 1) * 32)
                pe.wait_ge(p_ready, c * B_IT + n + (C_EXP if n == SPLIT else 1))
                t.matmul(ps[:, EXP[n % C_EXP], :], KT[:, j, kt * P:(kt + 1) * P], QS[:, h, j, :],
                         start=True, stop=True).then_inc(b_ready, 1)

            def pv_batch(i, b, c):
                if b == 0:
                    pe.wait_ge(po_free, c * PAIRS + i + C_ONE)
                pe.wait_ge(p_ready, c * B_IT + i * B_STEP + (b + 1) * BATCH + C_EXP)
                for r4 in range(BATCH):
                    h, kt = r4 // 2, 2 * b + r4 % 2
                    col = (2 * (i % PAIRS) + h) * VW
                    mm = t.matmul(ps[32 * r4:32 * r4 + 32, PO, :], Vx[:, kt, col:col + 32],
                                  ring[:, (b * BATCH + r4) % PRING, :], start=(b == 0), stop=(b == NB - 1))
                mm.then_inc(pv_done, 1)

            def shared(w, c, last=False):
                s = shared_slot(w, last)
                if not last or w < PAIRS - 1:
                    pe.wait_ge(mp_ready, c * PAIRS + w + 2)
                slot_free(s, c)
                if not last or w < PAIRS - 1:
                    mm = t.transpose(psb[0:2 * 3 * CT, A0 + 2 * (s % 2) + 1, 0:P], mp[:, (w + 1) % 2, :],
                                     identb[:, :])
                if type(c) is not int or w > 0 or last:
                    pe.wait_ge(po_free, c * PAIRS + w + C_ONE)
                    for q in range(CT):
                        mm = t.matmul(ps[:, A0 + 2 * (s % 2), q * 2 * VW:(q + 1) * 2 * VW],
                                      outT[:, (w - 1) % 2, q * P:(q + 1) * P], pick[:, :], start=True, stop=True)
                mm.then_inc(a_ready, 1)

            def steps(w, start, stop, c, last=False):
                for k in range(start, stop):
                    exp_mm(w, k, c)
                    m = w * B_STEP + k + 2 * LEAD
                    if not last or m < 2 * A_IT:
                        max_mm(m, c)
                    if k % BATCH == BATCH - 1:
                        b = k // BATCH
                        if b:
                            pv_batch(w, b - 1, c)
                        elif w or type(c) is not int:
                            pv_batch(w - 1, NB - 1, c)
                    if k == SPLIT - 1:
                        shared(w, c, last)
                    if last and k % BATCH == BATCH - 1 and (w, k // BATCH) in LATE:
                        late(*LATE[w, k // BATCH])

            def late(kind, c):
                if kind == "O":
                    pe.wait_ge(taken, TURNED["T", c] + 1)
                    pe.wait_ge(x1_ready, c + NC + C_TWO)
                    for i in range(CT):
                        last = t.matmul(ps[:, late_banks(c)[1], i * D:(i + 1) * D], XOT[:, i * P:(i + 1) * P],
                                        WT[:, 3, :], start=True, stop=True)
                    last.then_inc(o_ready, 1)
                    return
                if kind == "T":
                    pe.wait_ge(xo_ready, c + 1)
                else:
                    pe.wait_ge(xn_ready, c + 2 * NC + 1)
                if TURNED[kind, c]:
                    pe.wait_ge(taken, TURNED[kind, c])
                else:
                    pe.wait_ge(a_free, (NC - 1) * SLOT_IT + shared_slot(PAIRS - 2, True) + 1)
                for i in range(CT):
                    last = t.transpose(ps[:, late_banks(c)[0], i * P:(i + 1) * P], (XO if kind == "T" else xn)[:, i, :],
                                       ident[:, :])
                last.then_inc(turned, 1)

            for m in range(TURNS):
                turn_terms(NC - 1, m)
                if m == 2:
                    pe.wait_ge(qk_ev, NT + C_TILE)
                    pe.wait_ge(t_ev, TURNS * NC // 2 + C_EXP)
                if m >= 2:
                    for x in range(2):
                        max_mm(2 * (m - 2) + x, 0)
            for m in range(2 * (TURNS - 2), 2 * LEAD):
                if m == A_STEP:
                    pe.wait_ge(t_ev, TURNS * NC + C_EXP)
                max_mm(m, 0)
                if m >= A_STEP and m % 2:
                    warm(1, EXP[1])
                if m == 2 * (LEAD - A_STEP) + SPLIT - 1:
                    shared(-1, 0)
            pe.wait_ge(xt_ready, 2 * NC + C_ONE)
            steps(0, 0, SPLIT, 0)
            with pe.Fori(0, NC - 1) as c:
                steps(0, SPLIT, B_STEP, c)
                for w in range(1, PAIRS):
                    steps(w, 0, B_STEP, c)
                steps(PAIRS, 0, SPLIT, c)
            steps(0, SPLIT, B_STEP, NC - 1, True)
            for w in range(1, PAIRS):
                steps(w, 0, B_STEP, NC - 1, True)
            pv_batch(PAIRS - 1, NB - 1, NC - 1)
            shared(PAIRS, NC - 1, True)

            pe.wait_ge(taken, TURNED["F", 2] + 1)
            pe.wait_ge(a_free, (NC - 1) * SLOT_IT + shared_slot(PAIRS - 1, True) + 1)
            expand_block(1, 0, 0)
            expand_block(1, 0, 1)
            pe.wait_ge(p_ready, NC * B_IT + C_EXP)
            late("T", 3)
            pe.wait_ge(a_free, (NC - 1) * SLOT_IT + shared_slot(PAIRS, True) + 1)
            pe.wait_ge(x1_ready, 2 * NC + C_TWO - 1)
            expand_block(1, 0, 2)
            expand_block(1, 0, 3)
            pe.wait_ge(po_free, NC * PAIRS + C_ONE)
            late("O", 3)
            expand(1, 1)
            late("F", 3)
            ffn(1)


_INS = ['L0_attn_x', 'L0_attn_wq', 'L0_attn_bq', 'L0_attn_wk', 'L0_attn_bk', 'L0_attn_wv', 'L0_attn_bv',
        'L0_attn_wo', 'L0_attn_bo', 'L0_ffn_W_fc', 'L0_ffn_ln_w', 'L0_ffn_ln_b', 'L0_ffn_W_proj']
_OUTS = [((1, S, D), 'float32')]


def kernel(**inputs):
    import numpy as _np
    import concourse.bacc as _bacc
    from concourse import mybir as _mybir
    from concourse.bass_utils import run_bass_kernel_spmd as _run

    nc = _bacc.Bacc("TRN2", target_bir_lowering=False, num_devices=1)
    arrays, args = {}, []
    for name in _INS:
        a = _np.ascontiguousarray(inputs[name])
        arrays[f"in_{name}_dram"] = a
        args.append(nc.dram_tensor(f"in_{name}_dram", a.shape, _mybir.dt.from_np(a.dtype), kind="ExternalInput").ap())
    for i, (shape, dtype) in enumerate(_OUTS):
        dt = _mybir.dt.from_np(_np.dtype(dtype))
        args.append(nc.dram_tensor(f"out_{i}_dram", shape, dt, kind="ExternalOutput").ap())
    macaron(nc, *args)
    r = _run(nc, [arrays], core_ids=[0])
    return r.results[0]["out_0_dram"]
```
